# Optimizing a Trainium2 kernel written in Bass

```python
import numpy as np
import jax
import jax.numpy as jnp

def _softmax(x, axis=-1):
    return jax.nn.softmax(x, axis=axis)

def _gelu(x):
    return jax.nn.gelu(x, approximate=True)

def _silu(x):
    return jax.nn.silu(x)

def _sigmoid(x):
    return jax.nn.sigmoid(x)

def _layernorm(x, axis=-1, eps=1e-05):
    m = jnp.mean(x, axis=axis, keepdims=True)
    v = jnp.var(x, axis=axis, keepdims=True)
    return (x - m) / jnp.sqrt(v + eps)

def _scatter_add(tgt, idx, src, axis=0):
    return tgt.at[idx].add(src)

def _segment_sum(src, seg, n):
    return jax.ops.segment_sum(src, seg, n)
kernel_name = 'mk_recurrent_d1_jaxref_r4_ec451e'

def setup_inputs(seed: int=0):
    np.random.seed(seed)
    _w = jnp.asarray

    def _L0_attn_setup():
        import jax, jax.numpy as jnp
        import numpy as np
        B, S, D = (4, 512, 256)
        key = jax.random.key(seed)
        kx, kq, kk, kv = jax.random.split(key, 4)
        bound = float(np.sqrt(6.0 / (D + D)))
        return {'x': jax.random.normal(kx, (B, S, D), dtype=jnp.float32), 'WQ': jax.random.uniform(kq, (D, D), jnp.float32, -bound, bound), 'WK': jax.random.uniform(kk, (D, D), jnp.float32, -bound, bound), 'WV': jax.random.uniform(kv, (D, D), jnp.float32, -bound, bound)}
    _L0_attn_in = _L0_attn_setup()

    def _L0_ffn_setup():
        import jax, jax.numpy as jnp
        import numpy as np
        E = 8
        G = 4
        LG = 2
        TOPK = 2
        ROUTE_SCALE = 1.0

        def _grouped_mm(x, w, counts):
            counts = counts.astype(jnp.int32)
            if hasattr(jax.lax, 'ragged_dot'):
                return jax.lax.ragged_dot(x, w, counts)
            offs = jnp.cumsum(counts)
            eid = jnp.searchsorted(offs, jnp.arange(x.shape[0]), side='right')
            oh = jax.nn.one_hot(eid, w.shape[0], dtype=x.dtype)
            return jnp.einsum('nd,ne,edh->nh', x, oh, w)
        key = jax.random.key(seed)
        ks = jax.random.split(key, 8)
        bs, slen, dim, hid, shid = (2, 512, 256, 128, 256)
        std = 0.02
        return {'x': jax.random.normal(ks[0], (bs, slen, dim), jnp.float32), 'w_gate': jax.random.normal(ks[1], (E, dim), jnp.float32) * std, 'w1': jax.random.normal(ks[2], (E, dim, hid), jnp.float32) * std, 'w2': jax.random.normal(ks[3], (E, hid, dim), jnp.float32) * std, 'w3': jax.random.normal(ks[4], (E, dim, hid), jnp.float32) * std, 'sw1': jax.random.normal(ks[5], (shid, dim), jnp.float32) * std, 'sw2': jax.random.normal(ks[6], (dim, shid), jnp.float32) * std, 'sw3': jax.random.normal(ks[7], (shid, dim), jnp.float32) * std, 'expert_bias': jnp.zeros((E,), jnp.float32)}
    _L0_ffn_in = _L0_ffn_setup()
    _d = {'L0_attn_x': _L0_attn_in['x'], 'L0_attn_WQ': _L0_attn_in['WQ'], 'L0_attn_WK': _L0_attn_in['WK'], 'L0_attn_WV': _L0_attn_in['WV'], 'L0_ffn_w_gate': _L0_ffn_in['w_gate'], 'L0_ffn_w1': _L0_ffn_in['w1'], 'L0_ffn_w2': _L0_ffn_in['w2'], 'L0_ffn_w3': _L0_ffn_in['w3'], 'L0_ffn_sw1': _L0_ffn_in['sw1'], 'L0_ffn_sw2': _L0_ffn_in['sw2'], 'L0_ffn_sw3': _L0_ffn_in['sw3'], 'L0_ffn_expert_bias': _L0_ffn_in['expert_bias']}
    _x0 = _d['L0_attn_x']
    _d['L0_attn_x'] = jax.random.normal(jax.random.fold_in(jax.random.key(seed), 1), (8, 512, 256), dtype=_x0.dtype)
    del _x0
    return _d

def reference(L0_attn_x, L0_attn_WQ, L0_attn_WK, L0_attn_WV, L0_ffn_w_gate, L0_ffn_w1, L0_ffn_w2, L0_ffn_w3, L0_ffn_sw1, L0_ffn_sw2, L0_ffn_sw3, L0_ffn_expert_bias):

    def _L0_attn_ref(x, WQ, WK, WV):
        import jax, jax.numpy as jnp
        import numpy as np
        B, S, D = (4, 512, 256)
        dk = WQ.shape[1]
        q = x @ WQ
        k = x @ WK
        v = x @ WV
        scores = jnp.einsum('bsd,btd->bst', q, k) / jnp.sqrt(jnp.asarray(dk, x.dtype))
        s = x.shape[1]
        causal = jnp.tril(jnp.ones((s, s), dtype=bool))
        scores = jnp.where(causal[None, :, :], scores, jnp.asarray(-jnp.inf, x.dtype))
        attention = jax.nn.softmax(scores, axis=-1)
        return jnp.einsum('bst,btd->bsd', attention, v)

    def _L0_ffn_ref(x, w_gate, w1, w2, w3, sw1, sw2, sw3, expert_bias):
        import jax, jax.numpy as jnp
        import numpy as np
        E = 8
        G = 4
        LG = 2
        TOPK = 2
        ROUTE_SCALE = 1.0

        def _grouped_mm(x, w, counts):
            counts = counts.astype(jnp.int32)
            if hasattr(jax.lax, 'ragged_dot'):
                return jax.lax.ragged_dot(x, w, counts)
            offs = jnp.cumsum(counts)
            eid = jnp.searchsorted(offs, jnp.arange(x.shape[0]), side='right')
            oh = jax.nn.one_hot(eid, w.shape[0], dtype=x.dtype)
            return jnp.einsum('nd,ne,edh->nh', x, oh, w)
        bs, slen, dim = x.shape
        xf = x.reshape(-1, dim)
        N = xf.shape[0]
        logits = xf @ w_gate.T
        scores = jax.nn.softmax(logits.astype(jnp.float32), axis=-1)
        original = scores
        s = (scores + expert_bias).reshape(N, G, E // G)
        group_scores = jax.lax.top_k(s, 2)[0].sum(-1)
        top_groups = jax.lax.top_k(group_scores, LG)[1]
        keep = jnp.zeros((N, G), bool).at[jnp.arange(N)[:, None], top_groups].set(True)
        masked = jnp.where(keep[:, :, None], s, -jnp.inf).reshape(N, E)
        topk_idx = jax.lax.top_k(masked, TOPK)[1]
        weights = (jnp.take_along_axis(original, topk_idx, axis=1) * ROUTE_SCALE).astype(x.dtype)
        counts = jnp.bincount(topk_idx.reshape(-1), length=E)
        flat_idx = topk_idx.reshape(-1)
        routed_in = xf[flat_idx]
        routed_in = (routed_in.astype(jnp.float32) * weights.reshape(-1, 1)).astype(x.dtype)
        h = jax.nn.silu(_grouped_mm(routed_in, w1, counts)) * _grouped_mm(routed_in, w3, counts)
        routed_out = _grouped_mm(h, w2, counts)
        shared = jax.nn.silu(xf @ sw1.T) * (xf @ sw3.T) @ sw2.T
        out = shared.at[flat_idx].add(routed_out)
        return out.reshape(bs, slen, dim)
    x = L0_attn_x
    xn = _layernorm(x, axis=-1)
    s = _L0_attn_ref(xn, L0_attn_WQ, L0_attn_WK, L0_attn_WV)
    g = _silu(_L0_ffn_ref(xn, L0_ffn_w_gate, L0_ffn_w1, L0_ffn_w2, L0_ffn_w3, L0_ffn_sw1, L0_ffn_sw2, L0_ffn_sw3, L0_ffn_expert_bias))
    x = x + s * g
    return x

_drawn_inputs = setup_inputs


def setup_inputs(seed=0):
    import zlib

    import numpy as np

    out = dict(_drawn_inputs(seed))
    spreads = {'L0_ffn_expert_bias': (0.0, 0.8)}
    factors = {'L0_attn_WQ': 8.0,
     'L0_attn_WK': 8.0,
     'L0_attn_WV': 8.0,
     'L0_ffn_w_gate': 8.0,
     'L0_ffn_w1': 8.0,
     'L0_ffn_w2': 8.0,
     'L0_ffn_w3': 8.0,
     'L0_ffn_sw1': 8.0,
     'L0_ffn_sw2': 8.0,
     'L0_ffn_sw3': 8.0}
    for name, (base, spread) in spreads.items():
        noise = np.random.default_rng([zlib.crc32(name.encode()), seed]).standard_normal(out[name].shape)
        drawn = base * np.exp(spread * noise) if base else spread * noise
        out[name] = jnp.asarray(drawn.astype(out[name].dtype))
    for name, factor in factors.items():
        out[name] = (out[name] * factor).astype(out[name].dtype)
    return out
```

```python
from contextlib import ExitStack

import concourse.bass as bass
import concourse.mybir as mybir

F32 = mybir.dt.float32
F32R = mybir.dt.float32r
BF16 = mybir.dt.bfloat16
ALU = mybir.AluOpType
ACT = mybir.ActivationFunctionType
AX = mybir.AxisListType

P = 128
EPS = 1e-5
MASKED = -3.0e38
DROPPED = 1.0e38


def build(nc, x, WQ, WK, WV, w_gate, w1, w2, w3, sw1, sw2, sw3, expert_bias, out):
    B, S, D = x.shape
    E, _, H = w1.shape
    T = S // P
    C = D // P
    NT = B * T
    NTOK = B * S
    VG = D + E
    K = 2
    NR = NT * K
    RB = NR // B
    RG = RB // 2
    PAIRS = E * E
    G = 4
    assert S == 512 and D == 256 and H == P and E == 8 and PAIRS == 64 and RG == 4

    with ExitStack() as ctx:
        def sb(name, shape, dt=F32):
            return ctx.enter_context(nc.sbuf_tensor(name, shape, dt))

        def sem(name):
            return ctx.enter_context(nc.semaphore(name))

        bank = [ctx.enter_context(nc.psum_tensor(f"bank{i}", [P, 512], F32)) for i in range(8)]

        xT_hi_all = sb("xT_hi_all", [P, B, C, S], F32R)
        xT_lo_all = sb("xT_lo_all", [P, B, C, S], F32R)
        attn_all = sb("attn_all", [P, NT, D])
        logits = sb("logits", [P, NT, E])

        ident = sb("ident", [P, P])
        ident_bf = sb("ident_bf", [P, P], BF16)
        causal_bf = sb("causal_bf", [P, P], BF16)
        zero_bf = sb("zero_bf", [P, D], BF16)
        ones_bf = sb("ones_bf", [P, P], BF16)
        fold = sb("fold", [P, PAIRS])
        neg_half = sb("neg_half", [P, T])
        eps = sb("eps", [P, T])
        iota_e = sb("iota_e", [P, NT, E])
        iota_em = sb("iota_em", [P, NT, E])
        iota_g, iota_gm = iota_e[:, :, 0:G], iota_em[:, :, 0:G]
        iota_pair = sb("iota_pair", [P, PAIRS])
        row_id = sb("row_id", [P, NT, K])
        partition = sb("partition", [P, 1])
        upper = sb("upper", [P, 1])
        pair_of_partition = sb("pair_of_partition", [P, 1])
        bias_bc = sb("bias_bc", [P, E])

        raw_qkv = sb("raw_qkv", [P, 3, C, D])
        raw_sw = sb("raw_sw", [P, 3, C, D])
        raw_gate = sb("raw_gate", [E, D])
        w13 = sb("w13", [P, 2, E, C, H])
        w2_sb = sb("w2_sb", [P, E, D])
        M_hi = sb("M_hi", [P, C, D], F32R)
        M_lo = sb("M_lo", [P, C, D], F32R)
        WVG_hi = sb("WVG_hi", [P, C, VG], F32R)
        WVG_lo = sb("WVG_lo", [P, C, VG], F32R)

        x_ring = sb("x_ring", [P, 2, T, D])
        xn = sb("xn", [P, T, D])
        probs = sb("probs", [P, 2, S])
        wqT = probs[:, 0, :].rearrange("p (c d) -> p c d", c=C)
        wkT = probs[:, 1, :].rearrange("p (c d) -> p c d", c=C)
        bn = sb("bn", [P, T, 6])
        mv = sb("mv", [P, T, 2])
        var_eps = sb("var_eps", [P, T])
        rstd = sb("rstd", [P, T])
        neg_max = sb("neg_max", [P, T])
        row_sum = sb("row_sum", [P, T])
        row_inv = sb("row_inv", [P, T])

        XT, VV, QT, PT = 2 * C * S, 2 * 2 * T * VG, 2 * C * S, 2 * 2 * S
        arena = sb("arena", [P, XT + VV + QT + PT], F32R)
        xT = arena[:, 0:XT].rearrange("p (h c s) -> p h c s", h=2, c=C)
        v_ring = arena[:, XT:XT + VV].rearrange("p (r h t d) -> p r h t d", r=2, h=2, t=T)
        qT = arena[:, XT + VV:XT + VV + QT].rearrange("p (h c s) -> p h c s", h=2, c=C)
        pT = arena[:, XT + VV + QT:].rearrange("p (r h s) -> p r h s", r=2, h=2)

        SW, HT, SS, OH, WO = 2 * 3 * C * D, 2 * C * S, 2 * RG * 2 * H, RG * P, 2 * RG * P
        assert SW + HT + SS + 2 * OH + WO + P <= XT + VV + QT + PT
        cut = [0]

        def part(n):
            cut[0] += n
            return arena[:, cut[0] - n:cut[0]]

        swT = part(SW).rearrange("p (h w c d) -> p h w c d", h=2, w=3, c=C)
        hT = part(HT).rearrange("p (h c s) -> p h c s", h=2, c=C)
        silu_split = part(SS).rearrange("p (g r h d) -> p g r h d", g=2, r=RG, h=2)
        one_hot_T = part(2 * OH).rearrange("p (g s) -> p g s", g=2)
        w_one_hot = part(WO).rearrange("p (g r s) -> p g r s", g=2, r=RG)
        A_stack = part(P)
        A_T = sb("A_T", [P, P], F32R)
        B_T = sb("B_T", [P, PAIRS])
        xn8 = sb("xn8", [P, C, 8])
        w13_flat = w13[:, :, :, :, :].rearrange("p a e c h -> p (a e c h)")
        h_silu = w13_flat[:, 0:C * S].rearrange("p (c s) -> p c s", c=C)
        h_full = w13_flat[:, C * S:2 * C * S].rearrange("p (c s) -> p c s", c=C)
        gate = w13_flat[:, 2 * C * S:3 * C * S].rearrange("p (t d) -> p t d", t=T)
        row_silu = w13_flat[:, 3 * C * S:4 * C * S].rearrange("p (g r d) -> p g r d", g=2, r=RG)
        stage = sb("stage", [P, 4, RB])
        stage_bf = sb("stage_bf", [P, RB], BF16)
        rows = sb("rows", [P, 4, NT, K])
        w_hi_r = sb("w_hi_r", [P, NT, K], F32R)

        raw_flat = raw_qkv[:, :, :, :].rearrange("p n c d -> p (n c d)")
        RT = NT * E
        ra, rb, rc, rs = [raw_flat[:, n * RT:(n + 1) * RT].rearrange("p (t e) -> p t e", e=E) for n in range(4)]
        picked = raw_flat[:, 4 * RT:(4 + K) * RT].rearrange("p (k t e) -> p k t e", k=K, e=E)
        picked_bf = sb("picked_bf", [P, NT, E], BF16)
        r1 = sb("r1", [P, NT])
        r2 = sb("r2", [P, NT])
        xn_flat = xn[:, :, :].rearrange("p t d -> p (t d)")
        gs, ga, gb, keep = [xn_flat[:, n * NT * G:(n + 1) * NT * G].rearrange("p (t g) -> p t g", g=G) for n in range(4)]
        e_of, g_of = [xn_flat[:, 4 * NT * G + n * NT * K:4 * NT * G + (n + 1) * NT * K].rearrange("p (t k) -> p t k", k=K)
                      for n in range(2)]
        counts = sb("counts", [P, E])
        offs = sb("offs", [P, E])

        shared8 = xn_flat[0:8, 3 * D:4 * D]
        sum_half, sum_w, pair_out = raw_flat[:, 0:H], raw_flat[:, H:2 * H], raw_flat[:, 2 * H:2 * H + PAIRS]
        out8 = probs[0:8, :, :].rearrange("p r (u d) -> p (r u) d", d=D)

        names = """w_loaded x_loaded out_stored x8_loaded out8_stored experts_loaded
            const_part const_ready wq_turned wq_ready wk_ready m_summed m_hi_ready m_ready wvg_hi wvg_lo wvg_ready gate_turned
            stats_part stats_done rstd_part rstd_done xn_done x_turned x_hi x_lo xT_copied
            v_summed v_hi v_lo logits_kept q_summed q_hi q_lo scores_done max_done exp_done
            p_turned pT_hi pT_lo pv_done inv_done attn_kept
            sw_turned sw_hi sw_ready xn8_ready a_summed b_kept a_split a_turned a_ready
            route shifted route_exp counted rows_ready w_hi_done
            hacc_zero h1_done h3_done h_silu_done h_mult_done h_hi h_lo o_done gate_done gated summed
            staged bc_done one_hot_done gathered rows_silu rows_hi rows_lo w_one_hot_done w_one_part accumulated shared8_kept
            picked_ready tail_v tail_p tail_a""".split()
        s = {n: sem(n) for n in names}

        x_v = x.rearrange("b (t p) d -> b p t d", p=P)
        out_v = out.rearrange("b (t p) d -> b p t d", p=P)
        block = ctx.enter_context(nc.Block())

        LOOP1 = B - 2

        def sequence(i):
            return 0 if isinstance(i, int) and i == B - 1 else i + 1

        @block.sync
        def _(sp):
            def load_x(b, slot_b):
                sp.dma_start(x_ring[:, slot_b % 2, :, :], x_v[b, :, :, :]).then_inc(s["x_loaded"], 16)

            load_x(0, 0)
            for n, w in enumerate((WQ, WK, WV)):
                sp.dma_start(raw_qkv[:, n, :, :], w.rearrange("(c p) k -> p c k", p=P)).then_inc(s["w_loaded"], 16)
            sp.dma_start(raw_gate[:, :], w_gate).then_inc(s["w_loaded"], 16)
            sp.wait_ge(s["x_loaded"], 16)
            load_x(1, 1)

            def copy_xT(b):
                sp.wait_ge(s["x_lo"], C * (b + 1))
                for h, dst in enumerate((xT_hi_all, xT_lo_all)):
                    sp.dma_start(dst[:, b, :, :].bitcast(F32), xT[:, h, :, :].bitcast(F32)).then_inc(s["xT_copied"], 16)

            def step(b):
                sp.wait_ge(s["xn_done"], b + 1)
                sp.wait_ge(s["x_loaded"], 16 * (b + 2))
                load_x(b + 2, b)
                copy_xT(b)

            step(0)
            for n, w in enumerate((sw1, sw3, sw2)):
                sp.dma_start(raw_sw[:, n, :, :], w.rearrange("(c p) k -> p c k", p=P)).then_inc(s["experts_loaded"], 16)
            for n, w in enumerate((w1, w3)):
                sp.dma_start(w13[:, n, :, :, :], w.rearrange("e (c p) h -> p e c h", p=P)).then_inc(s["experts_loaded"], 16)
            sp.dma_start(w2_sb[:, :, :], w2.rearrange("e h d -> h e d")).then_inc(s["experts_loaded"], 16)
            sp.dma_start(bias_bc[:, :], expert_bias.unsqueeze(0).to_broadcast([P, E])).then_inc(s["experts_loaded"], 16)
            with sp.Fori(1, LOOP1) as b:
                step(b)
            copy_xT(B - 2)
            copy_xT(B - 1)

            def reload_x(i):
                sp.wait_ge(s["x_loaded"], 16 * (B + i))
                load_x(sequence(i), i)

            sp.wait_ge(s["xn_done"], B)
            reload_x(0)
            reload_x(1)

            def store(i):
                sp.wait_ge(s["summed"], i + 1)
                sp.dma_start(out_v[sequence(i), :, :, :], x_ring[:, i % 2, :, :]).then_inc(s["out_stored"], 16)
                sp.wait_ge(s["out_stored"], 16 * (i + 1))

            with sp.Fori(0, B - 3) as i:
                store(i)
                reload_x(i + 2)
            store(B - 3)
            reload_x(B - 1)
            store(B - 2)
            sp.dma_start(out8[:, 0, :], x[0, 0:8, :]).then_inc(s["x8_loaded"], 16)
            store(B - 1)
            sp.wait_ge(s["tail_v"], 6)
            sp.dma_start(out[0, 0:8, :], out8[:, 3, :]).then_inc(s["out8_stored"], 16)
            sp.wait_ge(s["out8_stored"], 16)

        @block.gpsimd
        def _(pool):
            def made(ins):
                ins.then_inc(s["const_part"], 1)

            made(nc.gpsimd.memset(ident[:, :], 0.0))
            made(nc.gpsimd.memset(causal_bf[:, :], 0.0))
            made(nc.gpsimd.memset(fold[:, :], 0.0))
            made(nc.gpsimd.memset(neg_half[:, :], -0.5))
            made(nc.gpsimd.memset(eps[:, :], EPS))
            made(nc.gpsimd.memset(zero_bf[:, :], 0.0))
            made(nc.gpsimd.memset(ones_bf[:, :], 1.0))
            pool.wait_ge(s["const_part"], 7)
            made(nc.gpsimd.affine_select(out=ident[:, :], in_=ident[:, :], compare_op=ALU.not_equal, fill=1.0, base=0,
                                         pattern=[[-1, P]], channel_multiplier=1))
            made(nc.gpsimd.affine_select(out=causal_bf[:, :], in_=causal_bf[:, :], compare_op=ALU.is_ge, fill=MASKED,
                                         base=0, pattern=[[-1, P]], channel_multiplier=1))
            made(nc.gpsimd.affine_select(out=fold[:, :], in_=fold[:, :], compare_op=ALU.not_equal, fill=1.0, base=0,
                                         pattern=[[-1, PAIRS]], channel_multiplier=1))
            pool.wait_ge(s["const_part"], 10)
            made(nc.gpsimd.tensor_copy(ident_bf[:, :], ident[:, :]))
            nc.gpsimd.affine_select(out=fold[:, :], in_=fold[:, :], compare_op=ALU.not_equal, fill=1.0, base=-PAIRS,
                                    pattern=[[-1, PAIRS]], channel_multiplier=1).then_inc(s["const_ready"], 1)

            def rstd_of(b):
                pool.wait_ge(s["stats_done"], b + 1)
                nc.gpsimd.tensor_tensor(var_eps[:, :], mv[:, :, 1], eps[:, :], ALU.add).then_inc(s["rstd_part"], 1)
                pool.wait_ge(s["rstd_part"], b + 1)
                nc.gpsimd.tensor_tensor(rstd[:, :], var_eps[:, :], neg_half[:, :], ALU.pow).then_inc(s["rstd_done"], 1)

            rstd_of(0)
            rstd_of(1)

            def iota(dst, pattern, base, mult):
                nc.gpsimd.iota(dst, pattern=pattern, base=base, channel_multiplier=mult,
                               allow_small_or_imprecise_dtypes=True).then_inc(s["const_ready"], 1)

            iota(iota_e[:, :, :], [[0, NT], [1, E]], 0, 0)
            iota(iota_em[:, :, :], [[0, NT], [1, E]], -8, 0)
            iota(iota_pair[:, :], [[1, PAIRS]], 0, 0)
            iota(row_id[:, :, :], [[K * P, NT], [1, K]], 0, K)
            iota(partition[:, :], [[0, 1]], 0, 1)

            def keep_logits(b):
                pool.wait_ge(s["v_lo"], T * (b + 1))
                nc.gpsimd.tensor_tensor(logits[:, bass.ds(b * T, T), :], v_ring[:, b % 2, 0, :, D:VG].bitcast(F32),
                                        v_ring[:, b % 2, 1, :, D:VG].bitcast(F32), ALU.add).then_inc(s["logits_kept"], 1)

            keep_logits(0)
            with pool.Fori(0, LOOP1) as b:
                rstd_of(b + 2)
                keep_logits(b + 1)
            keep_logits(B - 1)

            pool.wait_ge(s["rows_ready"], 1)

            def stage_rows(i):
                if not isinstance(i, int) or i > 0:
                    pool.wait_ge(s["accumulated"], 2 * i - 1)
                    pool.wait_ge(s["rows_silu"], RB * i)
                    pool.wait_ge(s["bc_done"], 2 * i)
                    pool.wait_ge(s["w_one_hot_done"], 2 * i)
                src = rows[:, :, bass.ds(i * T, T), :]
                nc.gpsimd.tensor_copy(stage[:, :, :].rearrange("p f (t k) -> p f t k", k=K), src).then_inc(s["staged"], 1)
                pool.wait_ge(s["staged"], 2 * i + 1)
                nc.gpsimd.tensor_tensor(stage_bf[:, :], stage[:, 0, :], zero_bf[:, 0:RB], ALU.add).then_inc(s["staged"], 1)

            def one_hots(i, g):
                for j in range(RG):
                    r = g * RG + j
                    for h in range(2):
                        ins = nc.gpsimd.tensor_scalar(w_one_hot[:, g, j, h * PAIRS:(h + 1) * PAIRS], iota_pair[:, :],
                                                      stage[:, 0, r:r + 1], stage[:, 2 + h, r:r + 1],
                                                      ALU.is_equal, ALU.mult)
                ins.then_inc(s["w_one_hot_done"], 1)

            def add_x(i):
                pool.wait_ge(s["x_loaded"], 16 * (B + i + 1))
                pool.wait_ge(s["gated"], 2 * (i + 1))
                slot = x_ring[:, i % 2, :, :]
                nc.gpsimd.tensor_tensor(slot, slot, gate[:, :, :], ALU.add).then_inc(s["summed"], 1)

            stage_rows(0)
            one_hots(0, 0)
            one_hots(0, 1)
            with pool.Fori(1, B) as i:
                stage_rows(i)
                one_hots(i, 0)
                pool.wait_ge(s["accumulated"], 2 * i)
                add_x(i - 1)
                one_hots(i, 1)
            add_x(B - 1)

        @block.tensor
        def _(pe):
            def mm(dst, lhsT, rhs, start, stop, **kw):
                return nc.tensor.matmul(dst, lhsT, rhs, start=start, stop=stop, skip_group_check=True, **kw)

            def split_products(dst, terms):
                last = len(terms) - 1
                for n, (lh, ll, rh, rl) in enumerate(terms):
                    mm(dst, lh, rh, n == 0, False)
                    mm(dst, lh, rl, False, False)
                    ins = mm(dst, ll, rh, False, n == last)
                return ins

            pe.wait_ge(s["const_ready"], 1)
            pe.wait_ge(s["w_loaded"], 16 * 4)
            for n in range(2):
                for kc in range(C):
                    for dc in range(C):
                        ins = nc.tensor.transpose(bank[n][:, kc * D + dc * P:kc * D + (dc + 1) * P],
                                                  raw_qkv[:, n, dc, kc * P:(kc + 1) * P], ident[:, :])
                ins.then_inc(s["wq_turned"], 1)
            for dc in range(C):
                ins = nc.tensor.transpose(bank[2][:, dc * E:(dc + 1) * E], raw_gate[:, dc * P:(dc + 1) * P], ident[0:E, 0:E])
            ins.then_inc(s["gate_turned"], 1)
            pe.wait_ge(s["wq_ready"], 1)
            pe.wait_ge(s["wk_ready"], 1)
            for dc in range(C):
                for kc in range(C):
                    ins = mm(bank[3][:, dc * D:(dc + 1) * D], wqT[:, kc, dc * P:(dc + 1) * P], wkT[:, kc, :],
                             kc == 0, kc == C - 1)
            ins.then_inc(s["m_summed"], 1)

            sc_bank, pt_bank, pv_bank, v_bank, x_bank = bank[0:2], bank[2:4], bank[4], bank[5], bank[6:8]

            def turn_x(b):
                pe.wait_ge(s["xn_done"], b + 1)
                if not isinstance(b, int) or b > 0:
                    pe.wait_ge(s["q_lo"], C * b)
                for c in range(C):
                    for t in range(T):
                        ins = nc.tensor.transpose(x_bank[c][:, t * P:(t + 1) * P], xn[:, t, c * P:(c + 1) * P], ident[:, :])
                    ins.then_inc(s["x_turned"], 1)

            def values(b, t):
                if t == 0:
                    pe.wait_ge(s["x_lo"], C * (b + 1))
                if t > 0 or not isinstance(b, int) or b > 0:
                    pe.wait_ge(s["v_lo"], T * b + t)
                tok = slice(t * P, (t + 1) * P)
                split_products(v_bank[:, 0:VG], [(xT[:, 0, c, tok], xT[:, 1, c, tok], WVG_hi[:, c, :], WVG_lo[:, c, :])
                                                 for c in range(C)]).then_inc(s["v_summed"], 1)

            def queries(b, ec):
                pe.wait_ge(s["x_lo"], C * (b + 1))
                e = slice(ec * P, (ec + 1) * P)
                split_products(x_bank[ec][:, :], [(M_hi[:, c, e], M_lo[:, c, e], xT[:, 0, c, :], xT[:, 1, c, :])
                                                  for c in range(C)]).then_inc(s["q_summed"], 1)

            def scores(b, i):
                if i == 0:
                    pe.wait_ge(s["q_lo"], C * (b + 1))
                    pe.wait_ge(s["xT_copied"], 32 * (b + 1))
                if i >= 2 or not isinstance(b, int) or b > 0:
                    pe.wait_ge(s["exp_done"], T * b + i - 1)
                n = (i + 1) * P
                tok = slice(i * P, n)
                dst = sc_bank[i % 2][:, 0:n]
                split_products(dst, [(qT[:, 0, c, tok], qT[:, 1, c, tok], xT_hi_all[:, b, c, 0:n], xT_lo_all[:, b, c, 0:n])
                                     for c in range(C)])
                mm(sc_bank[i % 2][:, i * P:n], ident_bf[:, :], causal_bf[:, :], False, True).then_inc(s["scores_done"], 1)

            def turn_probs(b, i):
                pe.wait_ge(s["exp_done"], T * b + i + 1)
                if i >= 2 or not isinstance(b, int) or b > 0:
                    pe.wait_ge(s["pT_lo"], T * b + i - 1)
                for j in range(i + 1):
                    ins = nc.tensor.transpose(pt_bank[i % 2][:, j * P:(j + 1) * P], probs[:, i % 2, j * P:(j + 1) * P], ident[:, :])
                ins.then_inc(s["p_turned"], 1)

            def weigh(b, i):
                pe.wait_ge(s["pT_lo"], T * b + i + 1)
                if i > 0 or not isinstance(b, int) or b > 0:
                    pe.wait_ge(s["attn_kept"], T * b + i)
                split_products(pv_bank[:, 0:D], [(pT[:, i % 2, 0, j * P:(j + 1) * P], pT[:, i % 2, 1, j * P:(j + 1) * P],
                                                  v_ring[:, b % 2, 0, j, 0:D], v_ring[:, b % 2, 1, j, 0:D])
                                                 for j in range(i + 1)]).then_inc(s["pv_done"], 1)

            turn_x(0)
            pe.wait_ge(s["wvg_ready"], 1)
            pe.wait_ge(s["m_ready"], 1)
            for t in range(T):
                values(0, t)
            queries(0, 0)
            queries(0, 1)

            def step(b, project):
                scores(b, 0)
                scores(b, 1)
                if project:
                    turn_x(b + 1)
                turn_probs(b, 0)
                scores(b, 2)
                if project:
                    values(b + 1, 0)
                turn_probs(b, 1)
                weigh(b, 0)
                scores(b, 3)
                if project:
                    values(b + 1, 1)
                turn_probs(b, 2)
                weigh(b, 1)
                if project:
                    values(b + 1, 2)
                    queries(b + 1, 0)
                turn_probs(b, 3)
                weigh(b, 2)
                if project:
                    values(b + 1, 3)
                    queries(b + 1, 1)
                weigh(b, 3)

            step(0, True)
            with pe.Fori(1, LOOP1) as b:
                step(b, True)
            step(B - 2, True)
            step(B - 1, False)

            pe.wait_ge(s["experts_loaded"], 16 * 7)
            for n in range(3):
                pe.wait_ge(s["attn_kept"], T * B)
                for kc in range(C):
                    for dc in range(C):
                        ins = nc.tensor.transpose(bank[n][:, kc * D + dc * P:kc * D + (dc + 1) * P],
                                                  raw_sw[:, n, dc, kc * P:(kc + 1) * P], ident[:, :])
                ins.then_inc(s["sw_turned"], 1)
            pe.wait_ge(s["xn8_ready"], 1)
            for n in range(2):
                for g in range(E):
                    for c in range(C):
                        ins = mm(bank[3 + n][:, g * 8:(g + 1) * 8], w13[:, n, g, c, :], xn8[:, c, :], c == 0, c == C - 1)
                ins.then_inc(s["a_summed"], 1)
            pe.wait_ge(s["a_split"], 2)
            nc.tensor.transpose(bank[5][:, 0:P], A_T[:, :].bitcast(F32), ident[:, :]).then_inc(s["a_turned"], 1)
            mm(bank[7][:, 0:2 * H], zero_bf[:, 0:P], zero_bf[:, 0:2 * H], True, True)
            pe.wait_ge(s["picked_ready"], 1)
            mm(bank[6][:, 0:NT * E], ones_bf[:, :], picked_bf[:, :, :].rearrange("p t e -> p (t e)"), True, True
               ).then_inc(s["counted"], 1)

            h1_bank, h3_bank, o_bank, bc_bank, g_bank, acc_bank = bank[0:2], bank[2:4], bank[4], bank[5], bank[6], bank[7]

            def hidden(i, hc, w, dst, done):
                b = sequence(i)
                if not isinstance(i, int) or i > 0:
                    pe.wait_ge(s["h_mult_done"], C * i + hc - (C - 1))
                hid = slice(hc * P, (hc + 1) * P)
                split_products(dst[hc][:, :], [(swT[:, 0, w, c, hid], swT[:, 1, w, c, hid], xT_hi_all[:, b, c, :], xT_lo_all[:, b, c, :])
                                               for c in range(C)]).then_inc(s[done], 1)

            def shared_out(i, half):
                if half == 0:
                    pe.wait_ge(s["h_lo"], C * (i + 1))
                if half == 1 or not isinstance(i, int) or i > 0:
                    pe.wait_ge(s["gate_done"], 2 * i + half)
                if isinstance(i, int) and i == B - 1 and half == 1:
                    pe.wait_ge(s["shared8_kept"], 1)
                for u in range(2):
                    t = 2 * half + u
                    tok = slice(t * P, (t + 1) * P)
                    ins = split_products(o_bank[:, u * D:(u + 1) * D], [(hT[:, 0, c, tok], hT[:, 1, c, tok], swT[:, 0, 2, c, :], swT[:, 1, 2, c, :])
                                                                        for c in range(C)])
                ins.then_inc(s["o_done"], 1)

            def spread_pairs(i, g):
                if g == 0:
                    pe.wait_ge(s["staged"], 2 * (i + 1))
                if g == 1 or not isinstance(i, int) or i > 0:
                    pe.wait_ge(s["one_hot_done"], 2 * i + g)
                for j in range(RG):
                    r = g * RG + j
                    ins = mm(bc_bank[:, j * P:(j + 1) * P], stage_bf[:, r:r + 1].to_broadcast([P, P]), ident_bf[:, :], True, True)
                ins.then_inc(s["bc_done"], 1)

            def gather(i, g):
                pe.wait_ge(s["one_hot_done"], 2 * i + g + 1)
                if g == 1 or not isinstance(i, int) or i > 0:
                    pe.wait_ge(s["rows_silu"], RB * i + RG * g)
                for j in range(RG):
                    ins = mm(g_bank[:, j * H:(j + 1) * H], one_hot_T[:, g, j * P:(j + 1) * P], A_stack, True, True)
                ins.then_inc(s["gathered"], 1)

            def accumulate(i, g):
                pe.wait_ge(s["rows_lo"], 2 * i + g + 1)
                pe.wait_ge(s["w_one_hot_done"], 2 * i + g + 1)
                for j in range(RG):
                    ins = mm(acc_bank[:, 0:2 * H], w_one_hot[:, g, j, :],
                             silu_split[:, g, j, :, :].rearrange("p h d -> p (h d)"), False, True)
                ins.then_inc(s["accumulated"], 1)

            def step2(i, first=False):
                spread_pairs(i, 0)
                hidden(i, 0, 0, h1_bank, "h1_done")
                if not first:
                    accumulate(i - 1, 1)
                hidden(i, 0, 1, h3_bank, "h3_done")
                gather(i, 0)
                if not first:
                    shared_out(i - 1, 0)
                spread_pairs(i, 1)
                if not first:
                    shared_out(i - 1, 1)
                accumulate(i, 0)
                hidden(i, 1, 0, h1_bank, "h1_done")
                gather(i, 1)
                hidden(i, 1, 1, h3_bank, "h3_done")

            pe.wait_ge(s["rows_ready"], 1)
            pe.wait_ge(s["sw_ready"], 3)
            pe.wait_ge(s["a_ready"], 1)
            pe.wait_ge(s["b_kept"], 1)
            step2(0, first=True)
            with pe.Fori(1, B - 1) as i:
                step2(i)
            step2(B - 1)
            accumulate(B - 1, 1)
            shared_out(B - 1, 0)
            shared_out(B - 1, 1)
            pe.wait_ge(s["tail_v"], 2)
            mm(bc_bank[:, 0:PAIRS], sum_w[:, :], fold[:, :], True, True).then_inc(s["tail_p"], 1)
            pe.wait_ge(s["tail_v"], 3)
            for g in range(E):
                ins = mm(g_bank[0:8, 0:D], pair_out[:, g * 8:(g + 1) * 8], w2_sb[:, g, :], g == 0, g == E - 1)
            ins.then_inc(s["tail_p"], 1)

        @block.scalar
        def _(act):
            sc_bank, pt_bank, pv_bank, v_bank, x_bank = bank[0:2], bank[2:4], bank[4], bank[5], bank[6:8]

            def copy(dst, src, scale=1.0):
                return nc.scalar.activation(dst, src, ACT.Copy, scale=scale)

            act.wait_ge(s["w_loaded"], 16 * 4)
            copy(WVG_hi[:, :, 0:D], raw_qkv[:, 2, :, :]).then_inc(s["wvg_hi"], 1)
            act.wait_ge(s["wq_turned"], 2)
            copy(probs[:, 1, :], bank[1][:, :]).then_inc(s["wk_ready"], 1)
            act.wait_ge(s["gate_turned"], 1)
            copy(WVG_hi[:, :, D:VG], bank[2][:, 0:C * E].rearrange("p (c e) -> p c e", c=C)).then_inc(s["wvg_hi"], 1)
            act.wait_ge(s["m_summed"], 1)
            copy(M_hi[:, :, :].rearrange("p c d -> p (c d)"), bank[3][:, :], scale=D ** -0.5).then_inc(s["m_hi_ready"], 1)

            def x_high(b):
                if not isinstance(b, int) or b > 0:
                    act.wait_ge(s["xT_copied"], 32 * b)
                    act.wait_ge(s["v_summed"], T * b)
                    act.wait_ge(s["q_summed"], C * b)
                for c in range(C):
                    act.wait_ge(s["x_turned"], C * b + c + 1)
                    copy(xT[:, 0, c, :], x_bank[c][:, :]).then_inc(s["x_hi"], 1)

            def v_high(b, t):
                act.wait_ge(s["v_summed"], T * b + t + 1)
                copy(v_ring[:, b % 2, 0, t, :], v_bank[:, 0:VG]).then_inc(s["v_hi"], 1)

            def q_high(b, c):
                act.wait_ge(s["q_summed"], C * b + c + 1)
                if c == 0 and (not isinstance(b, int) or b > 0):
                    act.wait_ge(s["scores_done"], T * b)
                copy(qT[:, 0, c, :], x_bank[c][:, :]).then_inc(s["q_hi"], 1)

            def soft(b, i):
                act.wait_ge(s["max_done"], T * b + i + 1)
                if i >= 2 or not isinstance(b, int) or b > 0:
                    act.wait_ge(s["p_turned"], T * b + i - 1)
                if not isinstance(b, int) or b > 0:
                    act.wait_ge(s["inv_done"], T * b + i + 1 - T)
                n = (i + 1) * P
                nc.scalar.activation(probs[:, i % 2, 0:n], sc_bank[i % 2][:, 0:n], ACT.Exp, bias=neg_max[:, i:i + 1],
                                     accum_out=row_sum[:, i:i + 1]).then_inc(s["exp_done"], 1)

            def p_high(b, i):
                act.wait_ge(s["p_turned"], T * b + i + 1)
                if i >= 2 or not isinstance(b, int) or b > 0:
                    act.wait_ge(s["pv_done"], T * b + i - 1)
                n = (i + 1) * P
                copy(pT[:, i % 2, 0, 0:n], pt_bank[i % 2][:, 0:n]).then_inc(s["pT_hi"], 1)

            def keep_attn(b, i):
                act.wait_ge(s["pv_done"], T * b + i + 1)
                act.wait_ge(s["inv_done"], T * b + i + 1)
                copy(attn_all[:, b * T + i, :], pv_bank[:, 0:D], scale=row_inv[:, i:i + 1]).then_inc(s["attn_kept"], 1)

            x_high(0)
            for t in range(T):
                v_high(0, t)
            q_high(0, 0)
            q_high(0, 1)

            def step(b, project):
                soft(b, 0)
                soft(b, 1)
                if project:
                    x_high(b + 1)
                p_high(b, 0)
                soft(b, 2)
                if project:
                    v_high(b + 1, 0)
                p_high(b, 1)
                keep_attn(b, 0)
                soft(b, 3)
                if project:
                    v_high(b + 1, 1)
                p_high(b, 2)
                keep_attn(b, 1)
                if project:
                    v_high(b + 1, 2)
                    q_high(b + 1, 0)
                p_high(b, 3)
                keep_attn(b, 2)
                if project:
                    v_high(b + 1, 3)
                    q_high(b + 1, 1)
                keep_attn(b, 3)

            step(0, True)
            with act.Fori(1, LOOP1) as b:
                step(b, True)
            step(B - 2, True)
            step(B - 1, False)

            act.wait_ge(s["shifted"], 1)
            nc.scalar.activation(rb[:, :, :], ra[:, :, :], ACT.Exp).then_inc(s["route_exp"], 1)
            for n in range(3):
                act.wait_ge(s["sw_turned"], n + 1)
                copy(swT[:, 0, n, :, :].rearrange("p c d -> p (c d)"), bank[n][:, :]).then_inc(s["sw_hi"], 1)
            act.wait_ge(s["a_summed"], 1)
            copy(A_T[:, 0:PAIRS], bank[3][:, 0:PAIRS]).then_inc(s["a_split"], 1)
            act.wait_ge(s["a_summed"], 2)
            copy(B_T[:, :], bank[4][:, 0:PAIRS]).then_inc(s["b_kept"], 1)
            act.wait_ge(s["a_turned"], 1)
            copy(A_stack, bank[5][:, 0:P]).then_inc(s["a_ready"], 1)

            h1_bank, h3_bank, o_bank, bc_bank, g_bank, acc_bank = bank[0:2], bank[2:4], bank[4], bank[5], bank[6], bank[7]

            def silu_hidden(i, hc):
                act.wait_ge(s["h1_done"], C * i + hc + 1)
                if not isinstance(i, int) or i > 0:
                    act.wait_ge(s["h_mult_done"], C * i + hc - (C - 1))
                nc.scalar.activation(h_silu[:, hc, :], h1_bank[hc][:, :], ACT.Silu).then_inc(s["h_silu_done"], 1)

            def h_high(i, hc):
                act.wait_ge(s["h_mult_done"], C * i + hc + 1)
                if not isinstance(i, int) or i > 0:
                    act.wait_ge(s["o_done"], 2 * i)
                copy(hT[:, 0, hc, :], h_full[:, hc, :]).then_inc(s["h_hi"], 1)

            def silu_rows(i, g):
                act.wait_ge(s["gathered"], 2 * i + g + 1)
                act.wait_ge(s["staged"], 2 * (i + 1))
                if not isinstance(i, int) or i > 0:
                    act.wait_ge(s["rows_lo"], 2 * i + g - 1)
                for j in range(RG):
                    r = g * RG + j
                    nc.scalar.activation(row_silu[:, g, j, :], g_bank[:, j * H:(j + 1) * H], ACT.Silu,
                                         scale=stage[:, 1, r:r + 1]).then_inc(s["rows_silu"], 1)

            def rows_high(i, g):
                act.wait_ge(s["rows_silu"], RB * i + RG * (g + 1))
                if not isinstance(i, int) or i > 0:
                    act.wait_ge(s["accumulated"], 2 * i + g - 1)
                copy(silu_split[:, g, :, 0, :], row_silu[:, g, :, :]).then_inc(s["rows_hi"], 1)

            def silu_out(i, half):
                act.wait_ge(s["o_done"], 2 * i + half + 1)
                if not isinstance(i, int) or i > 0:
                    act.wait_ge(s["summed"], i)
                if isinstance(i, int) and i == B - 1 and half == 0:
                    copy(shared8[:, :], o_bank[0:8, 0:D]).then_inc(s["shared8_kept"], 1)
                nc.scalar.activation(gate[:, 2 * half:2 * half + 2, :].rearrange("p t d -> p (t d)"), o_bank[:, :],
                                     ACT.Silu).then_inc(s["gate_done"], 1)

            def step2(i, first=False):
                silu_hidden(i, 0)
                silu_rows(i, 0)
                rows_high(i, 0)
                if not first:
                    silu_out(i - 1, 0)
                    silu_out(i - 1, 1)
                h_high(i, 0)
                silu_hidden(i, 1)
                silu_rows(i, 1)
                rows_high(i, 1)
                h_high(i, 1)

            step2(0, first=True)
            with act.Fori(1, B - 1) as i:
                step2(i)
            step2(B - 1)
            silu_out(B - 1, 0)
            silu_out(B - 1, 1)
            act.wait_ge(s["tail_v"], 4)
            nc.scalar.activation(out8[:, 2, :], out8[:, 1, :], ACT.Silu).then_inc(s["tail_a"], 1)

        @block.vector
        def _(dve):
            sc_bank, pt_bank, pv_bank, v_bank, x_bank = bank[0:2], bank[2:4], bank[4], bank[5], bank[6:8]

            def low(dst, src, high):
                return nc.vector.tensor_tensor(dst, src, high.bitcast(F32), ALU.subtract)

            def normalise(b):
                dve.wait_ge(s["x_loaded"], 16 * (b + 1))
                if not isinstance(b, int) or b > 0:
                    dve.wait_ge(s["rstd_part"], b)
                for t in range(T):
                    ins = nc.vector.bn_stats(bn[:, t, :], x_ring[:, b % 2, t, :])
                ins.then_inc(s["stats_part"], 1)
                dve.wait_ge(s["const_ready"], 1)
                dve.wait_ge(s["stats_part"], b + 1)
                for t in range(T):
                    ins = nc.vector.bn_aggr(mv[:, t, :], bn[:, t, :])
                ins.then_inc(s["stats_done"], 1)

            def scale_x(b):
                dve.wait_ge(s["rstd_done"], b + 1)
                if not isinstance(b, int) or b > 0:
                    dve.wait_ge(s["x_turned"], C * b)
                for t in range(T):
                    ins = nc.vector.tensor_scalar(xn[:, t, :], x_ring[:, b % 2, t, :], mv[:, t, 0:1], rstd[:, t:t + 1],
                                                  ALU.subtract, ALU.mult)
                ins.then_inc(s["xn_done"], 1)

            def x_low(b):
                for c in range(C):
                    dve.wait_ge(s["x_hi"], C * b + c + 1)
                    low(xT[:, 1, c, :], x_bank[c][:, :], xT[:, 0, c, :]).then_inc(s["x_lo"], 1)

            def v_low(b, t):
                dve.wait_ge(s["v_hi"], T * b + t + 1)
                low(v_ring[:, b % 2, 1, t, :], v_bank[:, 0:VG], v_ring[:, b % 2, 0, t, :]).then_inc(s["v_lo"], 1)

            def q_low(b, c):
                dve.wait_ge(s["q_hi"], C * b + c + 1)
                low(qT[:, 1, c, :], x_bank[c][:, :], qT[:, 0, c, :]).then_inc(s["q_lo"], 1)

            def row_max(b, i):
                dve.wait_ge(s["scores_done"], T * b + i + 1)
                nc.vector.tensor_reduce(neg_max[:, i:i + 1], sc_bank[i % 2][:, 0:(i + 1) * P], AX.X, ALU.max,
                                        negate=True).then_inc(s["max_done"], 1)

            def p_low(b, i):
                dve.wait_ge(s["pT_hi"], T * b + i + 1)
                n = (i + 1) * P
                low(pT[:, i % 2, 1, 0:n], pt_bank[i % 2][:, 0:n], pT[:, i % 2, 0, 0:n]).then_inc(s["pT_lo"], 1)

            def invert(b, i):
                dve.wait_ge(s["exp_done"], T * b + i + 1)
                if not isinstance(b, int) or b > 0:
                    dve.wait_ge(s["attn_kept"], T * b + i + 1 - T)
                nc.vector.reciprocal(row_inv[:, i:i + 1], row_sum[:, i:i + 1]).then_inc(s["inv_done"], 1)

            normalise(0)
            dve.wait_ge(s["wq_turned"], 1)
            nc.vector.tensor_copy(probs[:, 0, :], bank[0][:, :]).then_inc(s["wq_ready"], 1)
            scale_x(0)
            dve.wait_ge(s["wvg_hi"], 1)
            low(WVG_lo[:, :, 0:D], raw_qkv[:, 2, :, :], WVG_hi[:, :, 0:D]).then_inc(s["wvg_lo"], 1)
            dve.wait_ge(s["wvg_hi"], 2)
            low(WVG_lo[:, :, D:VG], bank[2][:, 0:C * E].rearrange("p (c e) -> p c e", c=C),
                WVG_hi[:, :, D:VG]).then_inc(s["wvg_ready"], 1)
            dve.wait_ge(s["m_hi_ready"], 1)
            nc.vector.scalar_tensor_tensor(out=M_lo[:, :, :].rearrange("p c d -> p (c d)"), in0=bank[3][:, :], scalar=D ** -0.5,
                                           in1=M_hi[:, :, :].rearrange("p c d -> p (c d)").bitcast(F32),
                                           op0=ALU.mult, op1=ALU.subtract).then_inc(s["m_ready"], 1)
            x_low(0)
            normalise(1)
            for t in range(T):
                v_low(0, t)
            scale_x(1)
            q_low(0, 0)
            q_low(0, 1)

            def step(b, project, norm):
                row_max(b, 0)
                row_max(b, 1)
                if project:
                    x_low(b + 1)
                p_low(b, 0)
                invert(b, 0)
                if norm:
                    normalise(b + 2)
                row_max(b, 2)
                if project:
                    v_low(b + 1, 0)
                p_low(b, 1)
                invert(b, 1)
                row_max(b, 3)
                if project:
                    v_low(b + 1, 1)
                p_low(b, 2)
                invert(b, 2)
                if norm:
                    scale_x(b + 2)
                if project:
                    v_low(b + 1, 2)
                    q_low(b + 1, 0)
                p_low(b, 3)
                invert(b, 3)
                if project:
                    v_low(b + 1, 3)
                    q_low(b + 1, 1)

            step(0, True, True)
            with dve.Fori(1, LOOP1) as b:
                step(b, True, True)
            step(B - 2, True, False)
            step(B - 1, False, False)

            steps = [0]

            def link(ins):
                steps[0] += 1
                ins.then_inc(s["route"], 1)
                dve.wait_ge(s["route"], steps[0])

            def along(v, n):
                return v.unsqueeze(2).to_broadcast([P, NT, n])

            def pick(src, work, idx, idx_m, onehot, at, n):
                link(nc.vector.tensor_reduce(at, src, AX.X, ALU.max))
                link(nc.vector.tensor_tensor(work, src, along(at, n), ALU.is_equal))
                link(nc.vector.scalar_tensor_tensor(out=work, in0=work, scalar=-8.0, in1=idx, op0=ALU.mult, op1=ALU.add))
                link(nc.vector.tensor_reduce(at, work, AX.X, ALU.min))
                link(nc.vector.tensor_tensor(onehot, idx_m, along(at, n), ALU.is_equal))

            def without(dst, src, onehot):
                link(nc.vector.scalar_tensor_tensor(out=dst, in0=onehot, scalar=-DROPPED, in1=src, op0=ALU.mult, op1=ALU.add))

            dve.wait_ge(s["logits_kept"], B)
            dve.wait_ge(s["const_ready"], 6)
            link(nc.vector.tensor_scalar(upper[:, :], partition[:, :], float(PAIRS), float(-PAIRS), ALU.is_ge, ALU.mult))
            link(nc.vector.tensor_tensor(pair_of_partition[:, :], partition[:, :], upper[:, :], ALU.add))
            dve.wait_ge(s["experts_loaded"], 16 * 7)
            a3, b3, c3, s3 = ra[:, :, :], rb[:, :, :], rc[:, :, :], rs[:, :, :]
            link(nc.vector.tensor_reduce(r1[:, :], logits[:, :, :], AX.X, ALU.max))
            nc.vector.tensor_tensor(a3, logits[:, :, :], along(r1[:, :], E), ALU.subtract).then_inc(s["shifted"], 1)
            dve.wait_ge(s["xT_copied"], 32 * B)
            nc.vector.tensor_tensor(xn8[:, :, :], xT_hi_all[:, 0, :, 0:8].bitcast(F32), xT_lo_all[:, 0, :, 0:8].bitcast(F32),
                                    ALU.add).then_inc(s["xn8_ready"], 1)
            for n in range(3):
                dve.wait_ge(s["sw_hi"], n + 1)
                low(swT[:, 1, n, :, :].rearrange("p c d -> p (c d)"), bank[n][:, :],
                    swT[:, 0, n, :, :].rearrange("p c d -> p (c d)")).then_inc(s["sw_ready"], 1)
            dve.wait_ge(s["a_split"], 1)
            low(A_T[:, PAIRS:P], bank[3][:, 0:PAIRS], A_T[:, 0:PAIRS]).then_inc(s["a_split"], 1)
            dve.wait_ge(s["route_exp"], 1)
            link(nc.vector.reduce_sum(r1[:, :], b3, AX.X))
            link(nc.vector.reciprocal(r2[:, :], r1[:, :]))
            link(nc.vector.tensor_tensor(c3, b3, along(r2[:, :], E), ALU.mult))
            link(nc.vector.tensor_tensor(s3, c3, bias_bc[:, :].unsqueeze(1).to_broadcast([P, NT, E]), ALU.add))
            s4 = s3.rearrange("p t (g u) -> p t g u", u=2)
            link(nc.vector.tensor_tensor(gs[:, :, :], s4[:, :, :, 0], s4[:, :, :, 1], ALU.add))
            pick(gs[:, :, :], ga[:, :, :], iota_g[:, :, :], iota_gm[:, :, :], keep[:, :, :], r1[:, :], G)
            without(gs[:, :, :], gs[:, :, :], keep[:, :, :])
            pick(gs[:, :, :], ga[:, :, :], iota_g[:, :, :], iota_gm[:, :, :], gb[:, :, :], r1[:, :], G)
            link(nc.vector.tensor_tensor(keep[:, :, :], keep[:, :, :], gb[:, :, :], ALU.add))
            link(nc.vector.tensor_scalar(gb[:, :, :], keep[:, :, :], -1.0, DROPPED, ALU.add, ALU.mult))
            for u in range(2):
                link(nc.vector.tensor_tensor(a3.rearrange("p t (g u) -> p t g u", u=2)[:, :, :, u], s4[:, :, :, u], gb[:, :, :], ALU.add))
            for k in range(K):
                pick(a3, b3, iota_e[:, :, :], iota_em[:, :, :], picked[:, k, :, :], r1[:, :], E)
                link(nc.vector.tensor_scalar(e_of[:, :, k], r1[:, :], 8.0, None, ALU.add))
                if k + 1 < K:
                    without(a3, a3, picked[:, k, :, :])
            nc.vector.tensor_tensor(picked_bf[:, :, :], picked[:, 0, :, :], picked[:, 1, :, :], ALU.add).then_inc(s["picked_ready"], 1)
            for k in range(K):
                link(nc.vector.tensor_tensor(b3, c3, picked[:, k, :, :], ALU.mult))
                link(nc.vector.reduce_sum(rows[:, 1, :, k], b3, AX.X))
            link(nc.vector.tensor_copy(w_hi_r[:, :, :], rows[:, 1, :, :]))
            link(nc.vector.tensor_copy(rows[:, 2, :, :], w_hi_r[:, :, :].bitcast(F32)))
            link(nc.vector.tensor_tensor(rows[:, 3, :, :], rows[:, 1, :, :], rows[:, 2, :, :], ALU.subtract))
            dve.wait_ge(s["counted"], 1)
            link(nc.vector.reduce_sum(counts[:, :], bank[6][:, 0:NT * E].rearrange("p (t e) -> p e t", e=E), AX.X))
            link(nc.vector.tensor_copy(offs[:, 0:1], counts[:, 0:1]))
            for e in range(1, E - 1):
                link(nc.vector.tensor_tensor(offs[:, e:e + 1], offs[:, e - 1:e], counts[:, e:e + 1], ALU.add))
            link(nc.vector.tensor_scalar(g_of[:, :, :], row_id[:, :, :], offs[:, 0:1], None, ALU.is_ge))
            for e in range(1, E - 1):
                link(nc.vector.scalar_tensor_tensor(out=g_of[:, :, :], in0=row_id[:, :, :], scalar=offs[:, e:e + 1], in1=g_of[:, :, :],
                                                    op0=ALU.is_ge, op1=ALU.add))
            nc.vector.scalar_tensor_tensor(out=rows[:, 0, :, :], in0=g_of[:, :, :], scalar=float(E), in1=e_of[:, :, :],
                                           op0=ALU.mult, op1=ALU.add).then_inc(s["rows_ready"], 1)

            h1_bank, h3_bank, o_bank, bc_bank, g_bank, acc_bank = bank[0:2], bank[2:4], bank[4], bank[5], bank[6], bank[7]

            def one_hot(i, g):
                dve.wait_ge(s["bc_done"], 2 * i + g + 1)
                if not isinstance(i, int) or i > 0:
                    dve.wait_ge(s["gathered"], 2 * i + g - 1)
                nc.vector.tensor_scalar(one_hot_T[:, g, :], bc_bank[:, :], pair_of_partition[:, 0:1], None,
                                        ALU.is_equal).then_inc(s["one_hot_done"], 1)

            def h_mult(i, hc):
                dve.wait_ge(s["h_silu_done"], C * i + hc + 1)
                dve.wait_ge(s["h3_done"], C * i + hc + 1)
                nc.vector.tensor_tensor(h_full[:, hc, :], h3_bank[hc][:, :], h_silu[:, hc, :], ALU.mult).then_inc(s["h_mult_done"], 1)

            def h_low(i, hc):
                dve.wait_ge(s["h_hi"], C * i + hc + 1)
                low(hT[:, 1, hc, :], h_full[:, hc, :], hT[:, 0, hc, :]).then_inc(s["h_lo"], 1)

            def rows_low(i, g):
                dve.wait_ge(s["rows_hi"], 2 * i + g + 1)
                low(silu_split[:, g, :, 1, :], row_silu[:, g, :, :], silu_split[:, g, :, 0, :]).then_inc(s["rows_lo"], 1)

            def gate_attn(i, half):
                dve.wait_ge(s["gate_done"], 2 * i + half + 1)
                b = sequence(i)
                g2 = gate[:, 2 * half:2 * half + 2, :]
                nc.vector.tensor_tensor(g2, g2, attn_all[:, bass.ds(b * T + 2 * half, 2), :], ALU.mult).then_inc(s["gated"], 1)

            def step2(i, first=False):
                one_hot(i, 0)
                h_mult(i, 0)
                rows_low(i, 0)
                one_hot(i, 1)
                if not first:
                    gate_attn(i - 1, 0)
                    gate_attn(i - 1, 1)
                h_low(i, 0)
                h_mult(i, 1)
                rows_low(i, 1)
                h_low(i, 1)

            step2(0, first=True)
            with dve.Fori(1, B - 1) as i:
                step2(i)
            step2(B - 1)
            gate_attn(B - 1, 0)
            gate_attn(B - 1, 1)
            tail = [0]

            def tail_link(ins):
                tail[0] += 1
                ins.then_inc(s["tail_v"], 1)
                dve.wait_ge(s["tail_v"], tail[0])

            dve.wait_ge(s["accumulated"], 2 * B)
            tail_link(nc.vector.tensor_copy(sum_half[:, :], acc_bank[:, 0:H]))
            tail_link(nc.vector.tensor_tensor(sum_w[:, :], acc_bank[:, H:2 * H], sum_half[:, :], ALU.add))
            dve.wait_ge(s["tail_p"], 1)
            tail_link(nc.vector.tensor_tensor(pair_out[:, :], bc_bank[:, 0:PAIRS], B_T[:, :], ALU.mult))
            dve.wait_ge(s["tail_p"], 2)
            dve.wait_ge(s["shared8_kept"], 1)
            tail_link(nc.vector.tensor_tensor(out8[:, 1, :], g_bank[0:8, 0:D], shared8[:, :], ALU.add))
            dve.wait_ge(s["tail_a"], 1)
            dve.wait_ge(s["x8_loaded"], 16)
            tail_link(nc.vector.tensor_tensor(out8[:, 1, :], out8[:, 2, :], attn_all[0:8, 0, :], ALU.mult))
            tail_link(nc.vector.tensor_tensor(out8[:, 3, :], out8[:, 1, :], out8[:, 0, :], ALU.add))


NAMES = ["L0_attn_x", "L0_attn_WQ", "L0_attn_WK", "L0_attn_WV", "L0_ffn_w_gate", "L0_ffn_w1", "L0_ffn_w2", "L0_ffn_w3",
         "L0_ffn_sw1", "L0_ffn_sw2", "L0_ffn_sw3", "L0_ffn_expert_bias"]


def kernel(**inputs):
    import numpy as np
    import concourse.bacc as bacc
    from concourse.bass_utils import run_bass_kernel_spmd

    nc = bacc.Bacc("TRN2", target_bir_lowering=False, num_devices=1)
    arrays, args = {}, []
    for name in NAMES:
        a = np.ascontiguousarray(inputs[name])
        arrays[f"in_{name}"] = a
        args.append(nc.dram_tensor(f"in_{name}", a.shape, mybir.dt.from_np(a.dtype), kind="ExternalInput").ap())
    out = nc.dram_tensor("out", inputs["L0_attn_x"].shape, F32, kind="ExternalOutput").ap()
    build(nc, *args, out)
    r = run_bass_kernel_spmd(nc, [arrays], core_ids=[0])
    return r.results[0]["out"]
```

```python
from contextlib import ExitStack

import concourse.bass as bass
import concourse.mybir as mybir

F32 = mybir.dt.float32
F32R = mybir.dt.float32r
BF16 = mybir.dt.bfloat16
ALU = mybir.AluOpType
ACT = mybir.ActivationFunctionType
AX = mybir.AxisListType

P = 128
EPS = 1e-5
MASKED = -3.0e38
DROPPED = 1.0e38


def build(nc, x, WQ, WK, WV, w_gate, w1, w2, w3, sw1, sw2, sw3, expert_bias, out):
    B, S, D = x.shape
    E, _, H = w1.shape
    T = S // P
    C = D // P
    NT = B * T
    NTOK = B * S
    VG = D + E
    K = 2
    NR = NT * K
    RB = NR // B
    RG = RB // 2
    PAIRS = E * E
    G = 4
    assert S == 512 and D == 256 and H == P and E == 8 and PAIRS == 64 and RG == 4

    with ExitStack() as ctx:
        def sb(name, shape, dt=F32):
            return ctx.enter_context(nc.sbuf_tensor(name, shape, dt))

        def sem(name):
            return ctx.enter_context(nc.semaphore(name))

        bank = [ctx.enter_context(nc.psum_tensor(f"bank{i}", [P, 512], F32)) for i in range(8)]

        xT_hi_all = sb("xT_hi_all", [P, B, C, S], F32R)
        xT_lo_all = sb("xT_lo_all", [P, B, C, S], F32R)
        attn_all = sb("attn_all", [P, NT, D])
        logits = sb("logits", [P, NT, E])

        ident = sb("ident", [P, P])
        ident_bf = sb("ident_bf", [P, P], BF16)
        causal_bf = sb("causal_bf", [P, P], BF16)
        zero_bf = sb("zero_bf", [P, D], BF16)
        ones_bf = sb("ones_bf", [P, P], BF16)
        fold = sb("fold", [P, PAIRS])
        neg_half = sb("neg_half", [P, T])
        eps = sb("eps", [P, T])
        iota_e = sb("iota_e", [P, E])
        iota_em = sb("iota_em", [P, E])
        iota_pair = sb("iota_pair", [P, PAIRS])
        row_id = sb("row_id", [P, NT, K])
        partition = sb("partition", [P, 1])
        upper = sb("upper", [P, 1])
        pair_of_partition = sb("pair_of_partition", [P, 1])
        bias_bc = sb("bias_bc", [P, E])

        raw_qkv = sb("raw_qkv", [P, 3, C, D])
        raw_sw = sb("raw_sw", [P, 3, C, D])
        raw_gate = sb("raw_gate", [E, D])
        w13 = sb("w13", [P, 2, E, C, H])
        w2_sb = sb("w2_sb", [P, E, D])
        M_hi = sb("M_hi", [P, C, D], F32R)
        M_lo = sb("M_lo", [P, C, D], F32R)
        WVG_hi = sb("WVG_hi", [P, C, VG], F32R)
        WVG_lo = sb("WVG_lo", [P, C, VG], F32R)

        x_ring = sb("x_ring", [P, 2, T, D])
        xn = sb("xn", [P, T, D])
        probs = sb("probs", [P, 2, S])
        wqT = probs[:, 0, :].rearrange("p (c d) -> p c d", c=C)
        wkT = probs[:, 1, :].rearrange("p (c d) -> p c d", c=C)
        bn = sb("bn", [P, T, 6])
        mv = sb("mv", [P, T, 2])
        var_eps = sb("var_eps", [P, T])
        rstd = sb("rstd", [P, T])
        neg_max = sb("neg_max", [P, T])
        row_sum = sb("row_sum", [P, T])
        row_inv = sb("row_inv", [P, T])

        XT, VV, QT, PT = 2 * C * S, 2 * 2 * T * VG, 2 * C * S, 2 * 2 * S
        arena = sb("arena", [P, XT + VV + QT + PT], F32R)
        xT = arena[:, 0:XT].rearrange("p (h c s) -> p h c s", h=2, c=C)
        v_ring = arena[:, XT:XT + VV].rearrange("p (r h t d) -> p r h t d", r=2, h=2, t=T)
        qT = arena[:, XT + VV:XT + VV + QT].rearrange("p (h c s) -> p h c s", h=2, c=C)
        pT = arena[:, XT + VV + QT:].rearrange("p (r h s) -> p r h s", r=2, h=2)

        SW, HT, SS, OH, WO = 2 * 3 * C * D, 2 * C * S, 2 * RG * 2 * H, RG * P, 2 * RG * P
        assert SW + HT + SS + 2 * OH + WO + P <= XT + VV + QT + PT
        cut = [0]

        def part(n):
            cut[0] += n
            return arena[:, cut[0] - n:cut[0]]

        swT = part(SW).rearrange("p (h w c d) -> p h w c d", h=2, w=3, c=C)
        A_stack = part(P)
        assert cut[0] <= XT + VV // 2
        hT = part(HT).rearrange("p (h c s) -> p h c s", h=2, c=C)
        silu_split = part(SS).rearrange("p (g r h d) -> p g r h d", g=2, r=RG, h=2)
        one_hot_T = part(2 * OH).rearrange("p (g s) -> p g s", g=2)
        w_one_hot = part(WO).rearrange("p (g r s) -> p g r s", g=2, r=RG)
        A_T = sb("A_T", [P, P], F32R)
        B_T = sb("B_T", [P, PAIRS])
        xn8 = sb("xn8", [P, C, 8])
        w13_flat = w13[:, :, :, :, :].rearrange("p a e c h -> p (a e c h)")
        h_silu = w13_flat[:, 0:C * S].rearrange("p (c s) -> p c s", c=C)
        h_full = w13_flat[:, C * S:2 * C * S].rearrange("p (c s) -> p c s", c=C)
        gate = w13_flat[:, 2 * C * S:3 * C * S].rearrange("p (t d) -> p t d", t=T)
        row_silu = w13_flat[:, 3 * C * S:4 * C * S].rearrange("p (g r d) -> p g r d", g=2, r=RG)
        stage = sb("stage", [P, 4, RB])
        stage_bf = sb("stage_bf", [P, RB], BF16)
        rows = sb("rows", [P, 4, NT, K])
        w_hi_r = sb("w_hi_r", [P, NT, K], F32R)

        gs = sb("gs", [P, NT, G])
        l_max = sb("l_max", [P, NT])
        l_sum = sb("l_sum", [P, NT])
        l_inv = sb("l_inv", [P, NT])
        raw_flat = raw_qkv[:, :, :, :].rearrange("p n c d -> p (n c d)")
        RT = NT * E
        ra, rb, rc, rs = [raw_flat[:, n * RT:(n + 1) * RT].rearrange("p (t e) -> p t e", e=E) for n in range(4)]
        picked = raw_flat[:, 4 * RT:(4 + K) * RT].rearrange("p (k t e) -> p k t e", k=K, e=E)
        picked_bf = sb("picked_bf", [P, NT, E], BF16)
        r1 = sb("r1", [P, NT])
        xn_flat = xn[:, :, :].rearrange("p t d -> p (t d)")
        ga, gb, keep = [xn_flat[:, n * NT * G:(n + 1) * NT * G].rearrange("p (t g) -> p t g", g=G) for n in range(3)]
        e_of, g_of = [xn_flat[:, 4 * NT * G + n * NT * K:4 * NT * G + (n + 1) * NT * K].rearrange("p (t k) -> p t k", k=K)
                      for n in range(2)]
        ends = [sb(f"ends{n}", [P, E]) for n in range(4)]
        at_or_past = raw_flat[:, 0:NR * (E - 1)].rearrange("p (r e) -> p r e", e=E - 1)

        sum_half, sum_w, pair_out = raw_flat[:, 0:H], raw_flat[:, H:2 * H], raw_flat[:, 2 * H:2 * H + PAIRS]

        names = """w_loaded x_loaded out_stored last_stored experts_loaded
            const_part const_ready wq_turned wq_ready wk_ready m_summed m_hi_ready m_ready wvg_hi wvg_lo wvg_ready gate_turned
            stats_part stats_done rstd_part rstd_done xn_done x_turned x_hi x_lo xT_copied
            v_summed v_hi v_lo logits_kept q_summed q_hi q_lo scores_done max_done exp_done
            p_turned pT_hi pT_lo pv_done inv_done attn_kept
            sw_turned sw_hi sw_ready xn8_ready tables_summed b_kept a_split a_turned a_ready
            route logits_max shifted route_exp inv_sum scored counted rows_ready
            h1_done h3_done h_silu_done h_mult_done h_hi h_lo o_done gate_done gated summed
            staged bc_done one_hot_done gathered rows_silu rows_hi rows_lo w_one_hot_done accumulated0 accumulated1
            inv_part picked_ready wqk_loaded sum_part sum_ready folded pairs_ready last_gated last_summed bias_loaded""".split()
        s = {n: sem(n) for n in names}

        x_v = x.rearrange("b (t p) d -> b p t d", p=P)
        out_v = out.rearrange("b (t p) d -> b p t d", p=P)
        block = ctx.enter_context(nc.Block())

        LOOP1 = B - 2

        def sequence(i):
            return 0 if isinstance(i, int) and i == B - 1 else i + 1

        @block.sync
        def _(sp):
            def load_x(b, slot_b):
                sp.dma_start(x_ring[:, slot_b % 2, :, :], x_v[b, :, :, :]).then_inc(s["x_loaded"], 16)

            load_x(0, 0)
            for n, w in enumerate((WQ, WK)):
                sp.dma_start(raw_qkv[:, n, :, :], w.rearrange("(c p) k -> p c k", p=P)).then_inc(s["wqk_loaded"], 16)
            sp.dma_start(raw_qkv[:, 2, :, :], WV.rearrange("(c p) k -> p c k", p=P)).then_inc(s["w_loaded"], 16)
            sp.dma_start(raw_gate[:, :], w_gate).then_inc(s["w_loaded"], 16)
            sp.dma_start(bias_bc[:, :], expert_bias.unsqueeze(0).to_broadcast([P, E])).then_inc(s["bias_loaded"], 16)
            sp.wait_ge(s["x_loaded"], 16)
            load_x(1, 1)

            def copy_xT(b):
                sp.wait_ge(s["x_lo"], C * (b + 1))
                for h, dst in enumerate((xT_hi_all, xT_lo_all)):
                    sp.dma_start(dst[:, b, :, :].bitcast(F32), xT[:, h, :, :].bitcast(F32)).then_inc(s["xT_copied"], 16)

            def step(b):
                sp.wait_ge(s["xn_done"], b + 1)
                sp.wait_ge(s["x_loaded"], 16 * (b + 2))
                load_x(b + 2, b)
                copy_xT(b)

            step(0)
            for n, w in enumerate((sw1, sw3, sw2)):
                sp.dma_start(raw_sw[:, n, :, :], w.rearrange("(c p) k -> p c k", p=P)).then_inc(s["experts_loaded"], 16)
            for n, w in enumerate((w1, w3)):
                sp.dma_start(w13[:, n, :, :, :], w.rearrange("e (c p) h -> p e c h", p=P)).then_inc(s["experts_loaded"], 16)
            sp.dma_start(w2_sb[:, :, :], w2.rearrange("e h d -> h e d")).then_inc(s["experts_loaded"], 16)
            with sp.Fori(1, LOOP1) as b:
                step(b)
            copy_xT(B - 2)
            copy_xT(B - 1)

            def reload_x(i):
                sp.wait_ge(s["x_loaded"], 16 * (B + i))
                load_x(sequence(i), i)

            sp.wait_ge(s["xn_done"], B)
            reload_x(0)
            reload_x(1)

            def store(i):
                sp.wait_ge(s["summed"], i + 1)
                sp.dma_start(out_v[sequence(i), :, :, :], x_ring[:, i % 2, :, :]).then_inc(s["out_stored"], 16)
                sp.wait_ge(s["out_stored"], 16 * (i + 1))

            with sp.Fori(0, B - 3) as i:
                store(i)
                reload_x(i + 2)
            store(B - 3)
            reload_x(B - 1)
            store(B - 2)
            for half in range(2):
                sp.wait_ge(s["last_summed"], half + 1)
                t2 = slice(2 * half, 2 * half + 2)
                sp.dma_start(out_v[0, :, t2, :], x_ring[:, (B - 1) % 2, t2, :]).then_inc(s["last_stored"], 16)
            sp.wait_ge(s["last_stored"], 32)

        @block.gpsimd
        def _(pool):
            def made(ins):
                ins.then_inc(s["const_part"], 1)

            made(nc.gpsimd.memset(ident[:, :], 0.0))
            made(nc.gpsimd.memset(causal_bf[:, :], 0.0))
            made(nc.gpsimd.memset(fold[:, :], 0.0))
            made(nc.gpsimd.memset(neg_half[:, :], -0.5))
            made(nc.gpsimd.memset(eps[:, :], EPS))
            made(nc.gpsimd.memset(zero_bf[:, :], 0.0))
            made(nc.gpsimd.memset(ones_bf[:, :], 1.0))
            pool.wait_ge(s["const_part"], 7)
            made(nc.gpsimd.affine_select(out=ident[:, :], in_=ident[:, :], compare_op=ALU.not_equal, fill=1.0, base=0,
                                         pattern=[[-1, P]], channel_multiplier=1))
            made(nc.gpsimd.affine_select(out=causal_bf[:, :], in_=causal_bf[:, :], compare_op=ALU.is_ge, fill=MASKED,
                                         base=0, pattern=[[-1, P]], channel_multiplier=1))
            made(nc.gpsimd.affine_select(out=fold[:, :], in_=fold[:, :], compare_op=ALU.not_equal, fill=1.0, base=0,
                                         pattern=[[-1, PAIRS]], channel_multiplier=1))
            pool.wait_ge(s["const_part"], 10)
            made(nc.gpsimd.tensor_copy(ident_bf[:, :], ident[:, :]))
            nc.gpsimd.affine_select(out=fold[:, :], in_=fold[:, :], compare_op=ALU.not_equal, fill=1.0, base=-PAIRS,
                                    pattern=[[-1, PAIRS]], channel_multiplier=1).then_inc(s["const_ready"], 1)

            def rstd_of(b):
                pool.wait_ge(s["stats_done"], b + 1)
                nc.gpsimd.tensor_tensor(var_eps[:, :], mv[:, :, 1], eps[:, :], ALU.add).then_inc(s["rstd_part"], 1)
                pool.wait_ge(s["rstd_part"], b + 1)
                nc.gpsimd.tensor_tensor(rstd[:, :], var_eps[:, :], neg_half[:, :], ALU.pow).then_inc(s["rstd_done"], 1)

            rstd_of(0)
            rstd_of(1)

            def iota(dst, pattern, base, mult):
                nc.gpsimd.iota(dst, pattern=pattern, base=base, channel_multiplier=mult,
                               allow_small_or_imprecise_dtypes=True).then_inc(s["const_ready"], 1)

            iota(iota_e[:, :], [[1, E]], 0, 0)
            iota(iota_em[:, :], [[1, E]], -8, 0)
            iota(iota_pair[:, :], [[1, PAIRS]], 0, 0)
            iota(row_id[:, :, :], [[K * P, NT], [1, K]], 0, K)
            iota(partition[:, :], [[0, 1]], 0, 1)

            def keep_logits(b):
                pool.wait_ge(s["v_lo"], T * (b + 1))
                nc.gpsimd.tensor_tensor(logits[:, bass.ds(b * T, T), :], v_ring[:, b % 2, 0, :, D:VG].bitcast(F32),
                                        v_ring[:, b % 2, 1, :, D:VG].bitcast(F32), ALU.add).then_inc(s["logits_kept"], 1)

            def shift_logits(b):
                tiles = bass.ds(b * T, T)
                pool.wait_ge(s["logits_max"], b + 1)
                nc.gpsimd.tensor_tensor(ra[:, tiles, :], logits[:, tiles, :], l_max[:, tiles].unsqueeze(2).to_broadcast([P, T, E]),
                                        ALU.subtract).then_inc(s["shifted"], 1)

            def score(b):
                tiles = bass.ds(b * T, T)
                pool.wait_ge(s["inv_sum"], b + 1)
                nc.gpsimd.tensor_tensor(rc[:, tiles, :], rb[:, tiles, :], l_inv[:, tiles].unsqueeze(2).to_broadcast([P, T, E]),
                                        ALU.mult).then_inc(s["scored"], 1)
                pool.wait_ge(s["scored"], 3 * b + 1)
                nc.gpsimd.tensor_tensor(rs[:, tiles, :], rc[:, tiles, :], bias_bc[:, :].unsqueeze(1).to_broadcast([P, T, E]),
                                        ALU.add).then_inc(s["scored"], 1)
                pool.wait_ge(s["scored"], 3 * b + 2)
                both = rs[:, tiles, :].rearrange("p t (g u) -> p t g u", u=2)
                nc.gpsimd.tensor_tensor(gs[:, tiles, :], both[:, :, :, 0], both[:, :, :, 1], ALU.add).then_inc(s["scored"], 1)

            keep_logits(0)
            pool.wait_ge(s["bias_loaded"], 16)
            with pool.Fori(0, LOOP1) as b:
                shift_logits(b)
                rstd_of(b + 2)
                score(b)
                keep_logits(b + 1)
            shift_logits(B - 2)
            score(B - 2)
            keep_logits(B - 1)
            shift_logits(B - 1)
            score(B - 1)

            pool.wait_ge(s["rows_ready"], 1)

            def stage_rows(i):
                if not isinstance(i, int) or i > 0:
                    pool.wait_ge(s["rows_silu"], RB * i)
                    pool.wait_ge(s["bc_done"], 2 * i)
                    pool.wait_ge(s["w_one_hot_done"], 2 * i)
                src = rows[:, :, bass.ds(i * T, T), :]
                nc.gpsimd.tensor_copy(stage[:, :, :].rearrange("p f (t k) -> p f t k", k=K), src).then_inc(s["staged"], 1)
                pool.wait_ge(s["staged"], 2 * i + 1)
                nc.gpsimd.tensor_tensor(stage_bf[:, :], stage[:, 0, :], zero_bf[:, 0:RB], ALU.add).then_inc(s["staged"], 1)

            def add_x(i):
                pool.wait_ge(s["x_loaded"], 16 * (B + i + 1))
                pool.wait_ge(s["gated"], 2 * (i + 1))
                slot = x_ring[:, i % 2, :, :]
                nc.gpsimd.tensor_tensor(slot, slot, gate[:, :, :], ALU.add).then_inc(s["summed"], 1)

            stage_rows(0)
            with pool.Fori(1, B - 1) as i:
                stage_rows(i)
                add_x(i - 1)
            stage_rows(B - 1)
            add_x(B - 2)

        @block.tensor
        def _(pe):
            def mm(dst, lhsT, rhs, start, stop, **kw):
                return nc.tensor.matmul(dst, lhsT, rhs, start=start, stop=stop, skip_group_check=True, **kw)

            def split_products(dst, terms):
                last = len(terms) - 1
                for n, (lh, ll, rh, rl) in enumerate(terms):
                    mm(dst, lh, rh, n == 0, False)
                    mm(dst, lh, rl, False, False)
                    ins = mm(dst, ll, rh, False, n == last)
                return ins

            pe.wait_ge(s["const_ready"], 1)
            pe.wait_ge(s["wqk_loaded"], 16 * 2)
            for n in range(2):
                for kc in range(C):
                    for dc in range(C):
                        ins = nc.tensor.transpose(bank[n][:, kc * D + dc * P:kc * D + (dc + 1) * P],
                                                  raw_qkv[:, n, dc, kc * P:(kc + 1) * P], ident[:, :])
                ins.then_inc(s["wq_turned"], 1)
            pe.wait_ge(s["w_loaded"], 16 * 2)
            for dc in range(C):
                ins = nc.tensor.transpose(bank[2][:, dc * E:(dc + 1) * E], raw_gate[:, dc * P:(dc + 1) * P], ident[0:E, 0:E])
            ins.then_inc(s["gate_turned"], 1)
            sc_bank, pt_bank, pv_bank, v_bank, x_bank = bank[0:2], bank[2:4], bank[4], bank[5], bank[6:8]
            first_v_banks = [bank[5], bank[4], bank[2], bank[0]]

            def turn_x(b, c):
                pe.wait_ge(s["xn_done"], b + 1)
                if not isinstance(b, int) or b > 0:
                    pe.wait_ge(s["q_lo"], C * b)
                for t in range(T):
                    ins = nc.tensor.transpose(x_bank[c][:, t * P:(t + 1) * P], xn[:, t, c * P:(c + 1) * P], ident[:, :])
                ins.then_inc(s["x_turned"], 1)

            def values(b, t):
                tok = slice(t * P, (t + 1) * P)
                dst = v_bank
                if isinstance(b, int) and b == 0:
                    dst = first_v_banks[t]
                else:
                    pe.wait_ge(s["v_lo"], T * b + t)
                if t == 0:
                    pe.wait_ge(s["x_lo"], C * (b + 1))
                split_products(dst[:, 0:VG], [(xT[:, 0, c, tok], xT[:, 1, c, tok], WVG_hi[:, c, :], WVG_lo[:, c, :])
                                              for c in range(C)]).then_inc(s["v_summed"], 1)

            def queries(b, ec):
                pe.wait_ge(s["x_lo"], C * (b + 1))
                e = slice(ec * P, (ec + 1) * P)
                split_products(x_bank[ec][:, :], [(M_hi[:, c, e], M_lo[:, c, e], xT[:, 0, c, :], xT[:, 1, c, :])
                                                  for c in range(C)]).then_inc(s["q_summed"], 1)

            def scores(b, i):
                if i == 0:
                    pe.wait_ge(s["q_lo"], C * (b + 1))
                    pe.wait_ge(s["xT_copied"], 32 * (b + 1))
                if i >= 2 or not isinstance(b, int) or b > 0:
                    pe.wait_ge(s["exp_done"], T * b + i - 1)
                n = (i + 1) * P
                tok = slice(i * P, n)
                dst = sc_bank[i % 2][:, 0:n]
                split_products(dst, [(qT[:, 0, c, tok], qT[:, 1, c, tok], xT_hi_all[:, b, c, 0:n], xT_lo_all[:, b, c, 0:n])
                                     for c in range(C)])
                mm(sc_bank[i % 2][:, i * P:n], ident_bf[:, :], causal_bf[:, :], False, True).then_inc(s["scores_done"], 1)

            def turn_probs(b, i):
                pe.wait_ge(s["exp_done"], T * b + i + 1)
                if i >= 2 or not isinstance(b, int) or b > 0:
                    pe.wait_ge(s["pT_lo"], T * b + i - 1)
                for j in range(i + 1):
                    ins = nc.tensor.transpose(pt_bank[i % 2][:, j * P:(j + 1) * P], probs[:, i % 2, j * P:(j + 1) * P], ident[:, :])
                ins.then_inc(s["p_turned"], 1)

            def weigh(b, i):
                pe.wait_ge(s["pT_lo"], T * b + i + 1)
                if i > 0 or not isinstance(b, int) or b > 0:
                    pe.wait_ge(s["attn_kept"], T * b + i)
                split_products(pv_bank[:, 0:D], [(pT[:, i % 2, 0, j * P:(j + 1) * P], pT[:, i % 2, 1, j * P:(j + 1) * P],
                                                  v_ring[:, b % 2, 0, j, 0:D], v_ring[:, b % 2, 1, j, 0:D])
                                                 for j in range(i + 1)]).then_inc(s["pv_done"], 1)

            turn_x(0, 0)
            turn_x(0, 1)
            pe.wait_ge(s["wq_ready"], 1)
            pe.wait_ge(s["wk_ready"], 1)
            for dc in range(C):
                for kc in range(C):
                    ins = mm(bank[3][:, dc * D:(dc + 1) * D], wqT[:, kc, dc * P:(dc + 1) * P], wkT[:, kc, :],
                             kc == 0, kc == C - 1)
            ins.then_inc(s["m_summed"], 1)

            pe.wait_ge(s["wvg_ready"], 1)
            for t in range(T):
                values(0, t)
            pe.wait_ge(s["m_ready"], 1)
            queries(0, 0)
            queries(0, 1)

            def step(b):
                p = b + 1
                scores(b, 0)
                scores(b, 1)
                turn_x(p, 0)
                turn_x(p, 1)
                scores(b, 2)
                turn_probs(b, 0)
                scores(b, 3)
                turn_probs(b, 1)
                values(p, 0)
                queries(p, 0)
                weigh(b, 0)
                values(p, 1)
                turn_probs(b, 2)
                weigh(b, 1)
                turn_probs(b, 3)
                values(p, 2)
                queries(p, 1)
                weigh(b, 2)
                values(p, 3)
                weigh(b, 3)

            step(0)
            with pe.Fori(1, LOOP1) as b:
                step(b)
            step(B - 2)

            b = B - 1
            sw_bank = [x_bank[0], x_bank[1], v_bank]

            def turn_sw(n):
                if n == 0:
                    pe.wait_ge(s["experts_loaded"], 16 * 6)
                pe.wait_ge(*((s["q_lo"], C * B) if n < 2 else (s["v_lo"], T * B)))
                for kc in range(C):
                    for dc in range(C):
                        ins = nc.tensor.transpose(sw_bank[n][:, kc * D + dc * P:kc * D + (dc + 1) * P],
                                                  raw_sw[:, n, dc, kc * P:(kc + 1) * P], ident[:, :])
                ins.then_inc(s["sw_turned"], 1)

            table_bank = [x_bank[0], v_bank]

            def table(n):
                pe.wait_ge(s["xn8_ready"], 1)
                pe.wait_ge(s["sw_ready"], 1 + 2 * n)
                for g in range(E):
                    for c in range(C):
                        ins = mm(table_bank[n][:, g * 8:(g + 1) * 8], w13[:, n, g, c, :], xn8[:, c, :],
                                 c == 0, c == C - 1)
                ins.then_inc(s["tables_summed"], 1)

            scores(b, 0)
            scores(b, 1)
            turn_sw(0)
            turn_probs(b, 0)
            scores(b, 2)
            turn_sw(1)
            turn_probs(b, 1)
            scores(b, 3)
            weigh(b, 0)
            turn_sw(2)
            turn_probs(b, 2)
            weigh(b, 1)
            turn_probs(b, 3)
            weigh(b, 2)
            table(0)
            weigh(b, 3)
            table(1)
            pe.wait_ge(s["a_split"], 2)
            pe.wait_ge(s["sw_ready"], 2)
            nc.tensor.transpose(x_bank[1][:, 0:P], A_T[:, :].bitcast(F32), ident[:, :]).then_inc(s["a_turned"], 1)

            h1_bank, h3_bank, o_bank, bc_bank, g_bank, acc_bank = bank[0:2], bank[2:4], bank[4], bank[5], bank[6], bank[7]

            def hidden(i, hc, w, dst, done):
                b = sequence(i)
                if not isinstance(i, int) or i > 0:
                    pe.wait_ge(s["h_mult_done"], C * i + hc - (C - 1))
                hid = slice(hc * P, (hc + 1) * P)
                split_products(dst[hc][:, :], [(swT[:, 0, w, c, hid], swT[:, 1, w, c, hid], xT_hi_all[:, b, c, :], xT_lo_all[:, b, c, :])
                                               for c in range(C)]).then_inc(s[done], 1)

            def shared_out(i, half):
                if half == 0:
                    pe.wait_ge(s["h_lo"], C * (i + 1))
                if half == 1 or not isinstance(i, int) or i > 0:
                    pe.wait_ge(s["gate_done"], 2 * i + half)
                for u in range(2):
                    t = 2 * half + u
                    tok = slice(t * P, (t + 1) * P)
                    ins = split_products(o_bank[:, u * D:(u + 1) * D], [(hT[:, 0, c, tok], hT[:, 1, c, tok], swT[:, 0, 2, c, :], swT[:, 1, 2, c, :])
                                                                        for c in range(C)])
                    if isinstance(i, int) and i == B - 1 and t == 0:
                        pe.wait_ge(s["pairs_ready"], 1)
                        for g in range(E):
                            mm(o_bank[0:8, 0:D], pair_out[:, g * 8:(g + 1) * 8], w2_sb[:, g, :], False, g == E - 1)
                ins.then_inc(s["o_done"], 1)

            def spread_pairs(i, g):
                if g == 0:
                    pe.wait_ge(s["staged"], 2 * (i + 1))
                if g == 1 or not isinstance(i, int) or i > 0:
                    pe.wait_ge(s["one_hot_done"], 2 * i + g)
                for j in range(RG):
                    r = g * RG + j
                    ins = mm(bc_bank[:, j * P:(j + 1) * P], stage_bf[:, r:r + 1].to_broadcast([P, P]), ident_bf[:, :], True, True)
                ins.then_inc(s["bc_done"], 1)

            def gather(i, g):
                pe.wait_ge(s["one_hot_done"], 2 * i + g + 1)
                if g == 1 or not isinstance(i, int) or i > 0:
                    pe.wait_ge(s["rows_silu"], RB * i + RG * g)
                for j in range(RG):
                    ins = mm(g_bank[:, j * H:(j + 1) * H], one_hot_T[:, g, j * P:(j + 1) * P], A_stack, True, True)
                ins.then_inc(s["gathered"], 1)

            def accumulate(i, g):
                pe.wait_ge(s["rows_lo"], 2 * i + g + 1)
                pe.wait_ge(s["w_one_hot_done"], 2 * i + g + 1)
                for j in range(RG):
                    ins = mm(acc_bank[:, 0:2 * H], w_one_hot[:, g, j, :],
                             silu_split[:, g, j, :, :].rearrange("p h d -> p (h d)"), False, True)
                ins.then_inc(s[f"accumulated{g}"], 1)

            pe.wait_ge(s["sw_ready"], 3)
            pe.wait_ge(s["exp_done"], T * B)
            pe.wait_ge(s["pT_lo"], T * B)
            hidden(0, 0, 0, h1_bank, "h1_done")
            hidden(0, 0, 1, h3_bank, "h3_done")
            pe.wait_ge(s["a_ready"], 1)
            mm(acc_bank[:, 0:2 * H], zero_bf[:, 0:P], zero_bf[:, 0:2 * H], True, True)
            pe.wait_ge(s["b_kept"], 1)
            pe.wait_ge(s["picked_ready"], 1)
            mm(bc_bank[:, 0:NT * E], ones_bf[:, :], picked_bf[:, :, :].rearrange("p t e -> p (t e)"), True, True
               ).then_inc(s["counted"], 1)
            hidden(0, 1, 0, h1_bank, "h1_done")
            hidden(0, 1, 1, h3_bank, "h3_done")
            pe.wait_ge(s["attn_kept"], T * B)
            pe.wait_ge(s["rows_ready"], 1)
            spread_pairs(0, 0)
            gather(0, 0)
            spread_pairs(0, 1)
            gather(0, 1)
            accumulate(0, 0)

            def step2(i):
                hidden(i, 0, 0, h1_bank, "h1_done")
                hidden(i, 0, 1, h3_bank, "h3_done")
                shared_out(i - 1, 0)
                spread_pairs(i, 0)
                hidden(i, 1, 0, h1_bank, "h1_done")
                gather(i, 0)
                spread_pairs(i, 1)
                shared_out(i - 1, 1)
                hidden(i, 1, 1, h3_bank, "h3_done")
                gather(i, 1)
                accumulate(i, 0)
                accumulate(i - 1, 1)

            with pe.Fori(1, B - 1) as i:
                step2(i)
            i = B - 1
            spread_pairs(i, 0)
            hidden(i, 0, 0, h1_bank, "h1_done")
            gather(i, 0)
            spread_pairs(i, 1)
            accumulate(i - 1, 1)
            hidden(i, 0, 1, h3_bank, "h3_done")
            gather(i, 1)
            shared_out(i - 1, 0)
            accumulate(i, 0)
            shared_out(i - 1, 1)
            accumulate(i, 1)
            hidden(i, 1, 0, h1_bank, "h1_done")
            pe.wait_ge(s["sum_ready"], 1)
            mm(bc_bank[:, 0:PAIRS], sum_w, fold[:, :], True, True).then_inc(s["folded"], 1)
            hidden(i, 1, 1, h3_bank, "h3_done")
            shared_out(i, 0)
            shared_out(i, 1)

        @block.scalar
        def _(act):
            sc_bank, pt_bank, pv_bank, v_bank, x_bank = bank[0:2], bank[2:4], bank[4], bank[5], bank[6:8]
            first_v_banks = [bank[5], bank[4], bank[2], bank[0]]

            def copy(dst, src, scale=1.0):
                return nc.scalar.activation(dst, src, ACT.Copy, scale=scale)

            def x_high(b, c):
                if not isinstance(b, int) or b > 0:
                    act.wait_ge(s["xT_copied"], 32 * b)
                    act.wait_ge(s["v_summed"], T * b)
                    act.wait_ge(s["q_summed"], C * b)
                act.wait_ge(s["x_turned"], C * b + c + 1)
                copy(xT[:, 0, c, :], x_bank[c][:, :]).then_inc(s["x_hi"], 1)

            def v_high(b, t):
                src = first_v_banks[t] if isinstance(b, int) and b == 0 else v_bank
                act.wait_ge(s["v_summed"], T * b + t + 1)
                copy(v_ring[:, b % 2, 0, t, :], src[:, 0:VG]).then_inc(s["v_hi"], 1)

            def q_high(b, c):
                act.wait_ge(s["q_summed"], C * b + c + 1)
                if c == 0 and (not isinstance(b, int) or b > 0):
                    act.wait_ge(s["scores_done"], T * b)
                copy(qT[:, 0, c, :], x_bank[c][:, :]).then_inc(s["q_hi"], 1)

            def soft(b, i):
                act.wait_ge(s["max_done"], T * b + i + 1)
                if i >= 2 or not isinstance(b, int) or b > 0:
                    act.wait_ge(s["p_turned"], T * b + i - 1)
                if not isinstance(b, int) or b > 0:
                    act.wait_ge(s["inv_done"], T * b + i + 1 - T)
                n = (i + 1) * P
                nc.scalar.activation(probs[:, i % 2, 0:n], sc_bank[i % 2][:, 0:n], ACT.Exp, bias=neg_max[:, i:i + 1],
                                     accum_out=row_sum[:, i:i + 1]).then_inc(s["exp_done"], 1)

            def p_high(b, i):
                act.wait_ge(s["p_turned"], T * b + i + 1)
                if i >= 2 or not isinstance(b, int) or b > 0:
                    act.wait_ge(s["pv_done"], T * b + i - 1)
                n = (i + 1) * P
                copy(pT[:, i % 2, 0, 0:n], pt_bank[i % 2][:, 0:n]).then_inc(s["pT_hi"], 1)

            def keep_attn(b, i):
                act.wait_ge(s["pv_done"], T * b + i + 1)
                act.wait_ge(s["inv_done"], T * b + i + 1)
                copy(attn_all[:, b * T + i, :], pv_bank[:, 0:D], scale=row_inv[:, i:i + 1]).then_inc(s["attn_kept"], 1)

            def exp_logits(b):
                tiles = bass.ds(b * T, T)
                act.wait_ge(s["shifted"], b + 1)
                nc.scalar.activation(rb[:, tiles, :], ra[:, tiles, :], ACT.Exp).then_inc(s["route_exp"], 1)

            act.wait_ge(s["w_loaded"], 16 * 2)
            copy(WVG_hi[:, :, 0:D], raw_qkv[:, 2, :, :]).then_inc(s["wvg_hi"], 1)
            act.wait_ge(s["wq_turned"], 2)
            copy(probs[:, 1, :], bank[1][:, :]).then_inc(s["wk_ready"], 1)
            act.wait_ge(s["gate_turned"], 1)
            copy(WVG_hi[:, :, D:VG], bank[2][:, 0:C * E].rearrange("p (c e) -> p c e", c=C)).then_inc(s["wvg_hi"], 1)
            x_high(0, 0)
            x_high(0, 1)
            act.wait_ge(s["m_summed"], 1)
            copy(M_hi[:, :, :].rearrange("p c d -> p (c d)"), bank[3][:, :], scale=D ** -0.5).then_inc(s["m_hi_ready"], 1)
            for t in range(T):
                v_high(0, t)
            q_high(0, 0)
            q_high(0, 1)

            def step(b):
                p = b + 1
                soft(b, 0)
                x_high(p, 0)
                soft(b, 1)
                x_high(p, 1)
                p_high(b, 0)
                p_high(b, 1)
                exp_logits(b)
                v_high(p, 0)
                soft(b, 2)
                soft(b, 3)
                keep_attn(b, 0)
                v_high(p, 1)
                q_high(p, 0)
                p_high(b, 2)
                p_high(b, 3)
                v_high(p, 2)
                keep_attn(b, 1)
                q_high(p, 1)
                keep_attn(b, 2)
                v_high(p, 3)
                keep_attn(b, 3)

            step(0)
            with act.Fori(1, LOOP1) as b:
                step(b)
            step(B - 2)

            b = B - 1
            sw_bank = [x_bank[0], x_bank[1], v_bank]

            def sw_high(n):
                if n == 0:
                    act.wait_ge(s["xT_copied"], 32 * B)
                act.wait_ge(s["sw_turned"], n + 1)
                copy(swT[:, 0, n, :, :].rearrange("p c d -> p (c d)"), sw_bank[n][:, :]).then_inc(s["sw_hi"], 1)

            soft(b, 0)
            soft(b, 1)
            exp_logits(b)
            p_high(b, 0)
            sw_high(0)
            soft(b, 2)
            p_high(b, 1)
            sw_high(1)
            soft(b, 3)
            keep_attn(b, 0)
            p_high(b, 2)
            sw_high(2)
            p_high(b, 3)
            keep_attn(b, 1)
            keep_attn(b, 2)
            act.wait_ge(s["tables_summed"], 1)
            copy(A_T[:, 0:PAIRS], x_bank[0][:, 0:PAIRS]).then_inc(s["a_split"], 1)
            keep_attn(b, 3)
            act.wait_ge(s["tables_summed"], 2)
            copy(B_T[:, :], v_bank[:, 0:PAIRS]).then_inc(s["b_kept"], 1)
            act.wait_ge(s["a_turned"], 1)
            copy(A_stack, x_bank[1][:, 0:P]).then_inc(s["a_ready"], 1)

            h1_bank, h3_bank, o_bank, bc_bank, g_bank, acc_bank = bank[0:2], bank[2:4], bank[4], bank[5], bank[6], bank[7]

            def silu_hidden(i, hc):
                act.wait_ge(s["h1_done"], C * i + hc + 1)
                if not isinstance(i, int) or i > 0:
                    act.wait_ge(s["h_mult_done"], C * i + hc - (C - 1))
                nc.scalar.activation(h_silu[:, hc, :], h1_bank[hc][:, :], ACT.Silu).then_inc(s["h_silu_done"], 1)

            def h_high(i, hc):
                act.wait_ge(s["h_mult_done"], C * i + hc + 1)
                if not isinstance(i, int) or i > 0:
                    act.wait_ge(s["o_done"], 2 * i)
                copy(hT[:, 0, hc, :], h_full[:, hc, :]).then_inc(s["h_hi"], 1)

            def silu_rows(i, g):
                act.wait_ge(s["gathered"], 2 * i + g + 1)
                act.wait_ge(s["staged"], 2 * (i + 1))
                if not isinstance(i, int) or i > 0:
                    act.wait_ge(s["rows_lo"], 2 * i + g - 1)
                for j in range(RG):
                    r = g * RG + j
                    nc.scalar.activation(row_silu[:, g, j, :], g_bank[:, j * H:(j + 1) * H], ACT.Silu,
                                         scale=stage[:, 1, r:r + 1]).then_inc(s["rows_silu"], 1)

            def rows_high(i, g):
                act.wait_ge(s["rows_silu"], RB * i + RG * (g + 1))
                if not isinstance(i, int) or i > 0:
                    act.wait_ge(s[f"accumulated{g}"], i)
                copy(silu_split[:, g, :, 0, :], row_silu[:, g, :, :]).then_inc(s["rows_hi"], 1)

            def silu_out(i, half):
                act.wait_ge(s["o_done"], 2 * i + half + 1)
                if not isinstance(i, int) or i > 0:
                    act.wait_ge(s["summed"], i)
                nc.scalar.activation(gate[:, 2 * half:2 * half + 2, :].rearrange("p t d -> p (t d)"), o_bank[:, :],
                                     ACT.Silu).then_inc(s["gate_done"], 1)

            silu_hidden(0, 0)
            silu_hidden(0, 1)
            silu_rows(0, 0)
            rows_high(0, 0)
            h_high(0, 0)
            silu_rows(0, 1)
            rows_high(0, 1)
            h_high(0, 1)

            def step2(i):
                silu_hidden(i, 0)
                silu_out(i - 1, 0)
                silu_rows(i, 0)
                rows_high(i, 0)
                silu_hidden(i, 1)
                silu_out(i - 1, 1)
                h_high(i, 0)
                h_high(i, 1)
                silu_rows(i, 1)
                rows_high(i, 1)

            with act.Fori(1, B - 1) as i:
                step2(i)
            i = B - 1
            silu_hidden(i, 0)
            silu_rows(i, 0)
            rows_high(i, 0)
            silu_rows(i, 1)
            rows_high(i, 1)
            silu_out(i - 1, 0)
            silu_out(i - 1, 1)
            h_high(i, 0)
            silu_hidden(i, 1)
            h_high(i, 1)
            silu_out(i, 0)
            silu_out(i, 1)

        @block.vector
        def _(dve):
            sc_bank, pt_bank, pv_bank, v_bank, x_bank = bank[0:2], bank[2:4], bank[4], bank[5], bank[6:8]
            first_v_banks = [bank[5], bank[4], bank[2], bank[0]]

            def low(dst, src, high):
                return nc.vector.tensor_tensor(dst, src, high.bitcast(F32), ALU.subtract)

            def stats(b, t):
                if t == 0:
                    dve.wait_ge(s["x_loaded"], 16 * (b + 1))
                ins = nc.vector.bn_stats(bn[:, t, :], x_ring[:, b % 2, t, :])
                if t == T - 1:
                    ins.then_inc(s["stats_part"], 1)

            def mean_var(b):
                dve.wait_ge(s["const_ready"], 1)
                dve.wait_ge(s["stats_part"], b + 1)
                if not isinstance(b, int) or b > 0:
                    dve.wait_ge(s["rstd_part"], b)
                for t in range(T):
                    ins = nc.vector.bn_aggr(mv[:, t, :], bn[:, t, :])
                ins.then_inc(s["stats_done"], 1)

            def scale_x(b, t):
                if t == 0:
                    dve.wait_ge(s["rstd_done"], b + 1)
                    if not isinstance(b, int) or b > 0:
                        dve.wait_ge(s["x_turned"], C * b)
                ins = nc.vector.tensor_scalar(xn[:, t, :], x_ring[:, b % 2, t, :], mv[:, t, 0:1], rstd[:, t:t + 1],
                                              ALU.subtract, ALU.mult)
                if t == T - 1:
                    ins.then_inc(s["xn_done"], 1)

            def x_low(b, c):
                dve.wait_ge(s["x_hi"], C * b + c + 1)
                low(xT[:, 1, c, :], x_bank[c][:, :], xT[:, 0, c, :]).then_inc(s["x_lo"], 1)

            def v_low(b, t):
                src = first_v_banks[t] if isinstance(b, int) and b == 0 else v_bank
                dve.wait_ge(s["v_hi"], T * b + t + 1)
                low(v_ring[:, b % 2, 1, t, :], src[:, 0:VG], v_ring[:, b % 2, 0, t, :]).then_inc(s["v_lo"], 1)

            def q_low(b, c):
                dve.wait_ge(s["q_hi"], C * b + c + 1)
                low(qT[:, 1, c, :], x_bank[c][:, :], qT[:, 0, c, :]).then_inc(s["q_lo"], 1)

            def row_max(b, i):
                dve.wait_ge(s["scores_done"], T * b + i + 1)
                nc.vector.tensor_reduce(neg_max[:, i:i + 1], sc_bank[i % 2][:, 0:(i + 1) * P], AX.X, ALU.max,
                                        negate=True).then_inc(s["max_done"], 1)

            def p_low(b, i):
                dve.wait_ge(s["pT_hi"], T * b + i + 1)
                n = (i + 1) * P
                low(pT[:, i % 2, 1, 0:n], pt_bank[i % 2][:, 0:n], pT[:, i % 2, 0, 0:n]).then_inc(s["pT_lo"], 1)

            def invert(b, i):
                dve.wait_ge(s["exp_done"], T * b + i + 1)
                if not isinstance(b, int) or b > 0:
                    dve.wait_ge(s["attn_kept"], T * b + i + 1 - T)
                nc.vector.reciprocal(row_inv[:, i:i + 1], row_sum[:, i:i + 1]).then_inc(s["inv_done"], 1)

            def logits_max(b):
                dve.wait_ge(s["logits_kept"], b + 1)
                tiles = bass.ds(b * T, T)
                nc.vector.tensor_reduce(l_max[:, tiles], logits[:, tiles, :], AX.X, ALU.max).then_inc(s["logits_max"], 1)

            def logits_sum(b):
                dve.wait_ge(s["route_exp"], b + 1)
                tiles = bass.ds(b * T, T)
                nc.vector.tensor_reduce(l_sum[:, tiles], rb[:, tiles, :], AX.X, ALU.add).then_inc(s["inv_part"], 1)

            def logits_inv(b):
                dve.wait_ge(s["inv_part"], b + 1)
                tiles = bass.ds(b * T, T)
                nc.vector.reciprocal(l_inv[:, tiles], l_sum[:, tiles]).then_inc(s["inv_sum"], 1)

            for t in range(T):
                stats(0, t)
            mean_var(0)
            for t in range(T):
                scale_x(0, t)
            dve.wait_ge(s["wq_turned"], 1)
            nc.vector.tensor_copy(probs[:, 0, :], bank[0][:, :]).then_inc(s["wq_ready"], 1)
            dve.wait_ge(s["wvg_hi"], 1)
            low(WVG_lo[:, :, 0:D], raw_qkv[:, 2, :, :], WVG_hi[:, :, 0:D]).then_inc(s["wvg_lo"], 1)
            dve.wait_ge(s["wvg_hi"], 2)
            low(WVG_lo[:, :, D:VG], bank[2][:, 0:C * E].rearrange("p (c e) -> p c e", c=C),
                WVG_hi[:, :, D:VG]).then_inc(s["wvg_ready"], 1)
            x_low(0, 0)
            x_low(0, 1)
            dve.wait_ge(s["m_hi_ready"], 1)
            nc.vector.scalar_tensor_tensor(out=M_lo[:, :, :].rearrange("p c d -> p (c d)"), in0=bank[3][:, :], scalar=D ** -0.5,
                                           in1=M_hi[:, :, :].rearrange("p c d -> p (c d)").bitcast(F32),
                                           op0=ALU.mult, op1=ALU.subtract).then_inc(s["m_ready"], 1)
            for t in range(T):
                stats(1, t)
            mean_var(1)
            for t in range(T):
                v_low(0, t)
            for t in range(T):
                scale_x(1, t)
            q_low(0, 0)
            q_low(0, 1)

            def step(b, norm=True):
                p = b + 1
                n = b + 2
                if norm:
                    stats(n, 0)
                row_max(b, 0)
                logits_max(b)
                if norm:
                    stats(n, 1)
                row_max(b, 1)
                if norm:
                    stats(n, 2)
                invert(b, 0)
                x_low(p, 0)
                x_low(p, 1)
                if norm:
                    stats(n, 3)
                row_max(b, 2)
                row_max(b, 3)
                p_low(b, 0)
                v_low(p, 0)
                if norm:
                    mean_var(n)
                p_low(b, 1)
                invert(b, 1)
                v_low(p, 1)
                invert(b, 2)
                logits_sum(b)
                if norm:
                    scale_x(n, 0)
                logits_inv(b)
                if norm:
                    scale_x(n, 1)
                    scale_x(n, 2)
                p_low(b, 2)
                q_low(p, 0)
                v_low(p, 2)
                p_low(b, 3)
                q_low(p, 1)
                v_low(p, 3)
                invert(b, 3)
                if norm:
                    scale_x(n, 3)

            step(0)
            with dve.Fori(1, LOOP1) as b:
                step(b)
            step(B - 2, norm=False)

            steps = [0]

            def link(ins):
                steps[0] += 1
                ins.then_inc(s["route"], 1)
                dve.wait_ge(s["route"], steps[0])

            def along(v, n):
                return v.unsqueeze(2).to_broadcast([P, NT, n])

            def index(v, n):
                return v[:, 0:n].unsqueeze(1).to_broadcast([P, NT, n])

            def pick(src, work, onehot, at, n):
                link(nc.vector.tensor_reduce(at, src, AX.X, ALU.max))
                link(nc.vector.tensor_tensor(work, src, along(at, n), ALU.is_equal))
                link(nc.vector.scalar_tensor_tensor(out=work, in0=work, scalar=-8.0, in1=index(iota_e, n), op0=ALU.mult, op1=ALU.add))
                link(nc.vector.tensor_reduce(at, work, AX.X, ALU.min))
                link(nc.vector.tensor_tensor(onehot, index(iota_em, n), along(at, n), ALU.is_equal))

            def without(dst, src, onehot):
                link(nc.vector.scalar_tensor_tensor(out=dst, in0=onehot, scalar=-DROPPED, in1=src, op0=ALU.mult, op1=ALU.add))

            b = B - 1
            sw_bank = [x_bank[0], x_bank[1], v_bank]

            def sw_low(n):
                dve.wait_ge(s["sw_hi"], n + 1)
                low(swT[:, 1, n, :, :].rearrange("p c d -> p (c d)"), sw_bank[n][:, :],
                    swT[:, 0, n, :, :].rearrange("p c d -> p (c d)")).then_inc(s["sw_ready"], 1)

            row_max(b, 0)
            logits_max(b)
            row_max(b, 1)
            nc.vector.tensor_tensor(xn8[:, :, :], xT_hi_all[:, 0, :, 0:8].bitcast(F32), xT_lo_all[:, 0, :, 0:8].bitcast(F32),
                                    ALU.add).then_inc(s["xn8_ready"], 1)
            invert(b, 0)
            logits_sum(b)
            p_low(b, 0)
            logits_inv(b)
            row_max(b, 2)
            sw_low(0)
            invert(b, 1)
            p_low(b, 1)
            row_max(b, 3)
            sw_low(1)
            invert(b, 2)
            p_low(b, 2)
            sw_low(2)
            dve.wait_ge(s["const_ready"], 6)
            link(nc.vector.tensor_scalar(upper[:, :], partition[:, :], float(PAIRS), float(-PAIRS), ALU.is_ge, ALU.mult))
            link(nc.vector.tensor_tensor(pair_of_partition[:, :], partition[:, :], upper[:, :], ALU.add))
            invert(b, 3)
            p_low(b, 3)
            dve.wait_ge(s["scored"], 3 * B)
            a3, b3, c3, s3 = ra[:, :, :], rb[:, :, :], rc[:, :, :], rs[:, :, :]
            s4 = s3.rearrange("p t (g u) -> p t g u", u=2)
            pick(gs[:, :, :], ga[:, :, :], keep[:, :, :], r1[:, :], G)
            without(gs[:, :, :], gs[:, :, :], keep[:, :, :])
            dve.wait_ge(s["a_split"], 1)
            low(A_T[:, PAIRS:P], x_bank[0][:, 0:PAIRS], A_T[:, 0:PAIRS]).then_inc(s["a_split"], 1)
            pick(gs[:, :, :], ga[:, :, :], gb[:, :, :], r1[:, :], G)
            link(nc.vector.tensor_tensor(keep[:, :, :], keep[:, :, :], gb[:, :, :], ALU.add))
            link(nc.vector.tensor_scalar(gb[:, :, :], keep[:, :, :], -1.0, DROPPED, ALU.add, ALU.mult))
            for u in range(2):
                ins = nc.vector.tensor_tensor(a3.rearrange("p t (g u) -> p t g u", u=2)[:, :, :, u], s4[:, :, :, u], gb[:, :, :], ALU.add)
            link(ins)
            for k in range(K):
                pick(a3, b3, picked[:, k, :, :], r1[:, :], E)
                link(nc.vector.tensor_scalar(e_of[:, :, k], r1[:, :], 8.0, None, ALU.add))
                if k + 1 < K:
                    without(a3, a3, picked[:, k, :, :])
            nc.vector.tensor_tensor(picked_bf[:, :, :], picked[:, 0, :, :], picked[:, 1, :, :], ALU.add).then_inc(s["picked_ready"], 1)
            for k in range(K):
                link(nc.vector.tensor_tensor(b3, c3, picked[:, k, :, :], ALU.mult))
                link(nc.vector.reduce_sum(rows[:, 1, :, k], b3, AX.X))
            link(nc.vector.tensor_copy(w_hi_r[:, :, :], rows[:, 1, :, :]))
            link(nc.vector.tensor_copy(rows[:, 2, :, :], w_hi_r[:, :, :].bitcast(F32)))
            link(nc.vector.tensor_tensor(rows[:, 3, :, :], rows[:, 1, :, :], rows[:, 2, :, :], ALU.subtract))
            dve.wait_ge(s["counted"], 1)
            link(nc.vector.reduce_sum(ends[0][:, :], bank[5][:, 0:NT * E].rearrange("p (t e) -> p e t", e=E), AX.X))
            for n, d in enumerate((1, 2, 4)):
                nc.vector.tensor_copy(ends[n + 1][:, 0:d], ends[n][:, 0:d])
                link(nc.vector.tensor_tensor(ends[n + 1][:, d:E], ends[n][:, d:E], ends[n][:, 0:E - d], ALU.add))
            row_ids = row_id[:, :, :].rearrange("p t k -> p (t k)")
            link(nc.vector.tensor_tensor(at_or_past, row_ids.unsqueeze(2).to_broadcast([P, NR, E - 1]),
                                         ends[3][:, 0:E - 1].unsqueeze(1).to_broadcast([P, NR, E - 1]), ALU.is_ge))
            link(nc.vector.reduce_sum(g_of.rearrange("p t k -> p (t k)"), at_or_past, AX.X))
            nc.vector.scalar_tensor_tensor(out=rows[:, 0, :, :], in0=g_of[:, :, :], scalar=float(E), in1=e_of[:, :, :],
                                           op0=ALU.mult, op1=ALU.add).then_inc(s["rows_ready"], 1)

            h1_bank, h3_bank, o_bank, bc_bank, g_bank, acc_bank = bank[0:2], bank[2:4], bank[4], bank[5], bank[6], bank[7]

            def weight_one_hots(i, g):
                dve.wait_ge(s["staged"], 2 * (i + 1))
                if not isinstance(i, int) or i > 0:
                    dve.wait_ge(s[f"accumulated{g}"], i)
                for j in range(RG):
                    r = g * RG + j
                    for h in range(2):
                        ins = nc.vector.tensor_scalar(w_one_hot[:, g, j, h * PAIRS:(h + 1) * PAIRS], iota_pair[:, :],
                                                      stage[:, 0, r:r + 1], stage[:, 2 + h, r:r + 1],
                                                      ALU.is_equal, ALU.mult)
                ins.then_inc(s["w_one_hot_done"], 1)

            def one_hot(i, g):
                dve.wait_ge(s["bc_done"], 2 * i + g + 1)
                if not isinstance(i, int) or i > 0:
                    dve.wait_ge(s["gathered"], 2 * i + g - 1)
                nc.vector.tensor_scalar(one_hot_T[:, g, :], bc_bank[:, :], pair_of_partition[:, 0:1], None,
                                        ALU.is_equal).then_inc(s["one_hot_done"], 1)

            def h_mult(i, hc):
                dve.wait_ge(s["h_silu_done"], C * i + hc + 1)
                dve.wait_ge(s["h3_done"], C * i + hc + 1)
                if not isinstance(i, int) or i > 0:
                    dve.wait_ge(s["h_lo"], C * i + hc + 1 - C)
                nc.vector.tensor_tensor(h_full[:, hc, :], h3_bank[hc][:, :], h_silu[:, hc, :], ALU.mult).then_inc(s["h_mult_done"], 1)

            def h_low(i, hc):
                dve.wait_ge(s["h_hi"], C * i + hc + 1)
                low(hT[:, 1, hc, :], h_full[:, hc, :], hT[:, 0, hc, :]).then_inc(s["h_lo"], 1)

            def rows_low(i, g):
                dve.wait_ge(s["rows_hi"], 2 * i + g + 1)
                low(silu_split[:, g, :, 1, :], row_silu[:, g, :, :], silu_split[:, g, :, 0, :]).then_inc(s["rows_lo"], 1)

            def gate_attn(i, half):
                dve.wait_ge(s["gate_done"], 2 * i + half + 1)
                b = sequence(i)
                g2 = gate[:, 2 * half:2 * half + 2, :]
                return nc.vector.tensor_tensor(g2, g2, attn_all[:, bass.ds(b * T + 2 * half, 2), :], ALU.mult)

            weight_one_hots(0, 0)
            one_hot(0, 0)
            one_hot(0, 1)
            h_mult(0, 0)
            weight_one_hots(0, 1)
            rows_low(0, 0)
            h_mult(0, 1)
            h_low(0, 0)
            rows_low(0, 1)
            h_low(0, 1)

            def step2(i):
                h_mult(i, 0)
                one_hot(i, 0)
                gate_attn(i - 1, 0).then_inc(s["gated"], 1)
                weight_one_hots(i, 0)
                one_hot(i, 1)
                rows_low(i, 0)
                h_mult(i, 1)
                gate_attn(i - 1, 1).then_inc(s["gated"], 1)
                h_low(i, 0)
                h_low(i, 1)
                weight_one_hots(i, 1)
                rows_low(i, 1)

            with dve.Fori(1, B - 1) as i:
                step2(i)
            i = B - 1
            one_hot(i, 0)
            weight_one_hots(i, 0)
            one_hot(i, 1)
            h_mult(i, 0)
            rows_low(i, 0)
            weight_one_hots(i, 1)
            rows_low(i, 1)
            gate_attn(i - 1, 0).then_inc(s["gated"], 1)
            gate_attn(i - 1, 1).then_inc(s["gated"], 1)
            h_low(i, 0)
            dve.wait_ge(s["accumulated0"], B)
            dve.wait_ge(s["accumulated1"], B)
            nc.vector.tensor_copy(sum_half, acc_bank[:, 0:H]).then_inc(s["sum_part"], 1)
            dve.wait_ge(s["sum_part"], 1)
            nc.vector.tensor_tensor(sum_w, acc_bank[:, H:2 * H], sum_half, ALU.add).then_inc(s["sum_ready"], 1)
            h_mult(i, 1)
            dve.wait_ge(s["folded"], 1)
            nc.vector.tensor_tensor(pair_out, bc_bank[:, 0:PAIRS], B_T[:, :], ALU.mult).then_inc(s["pairs_ready"], 1)
            h_low(i, 1)
            dve.wait_ge(s["x_loaded"], 16 * 2 * B)
            for half in range(2):
                gate_attn(i, half).then_inc(s["last_gated"], 1)
                dve.wait_ge(s["last_gated"], half + 1)
                slot = x_ring[:, i % 2, 2 * half:2 * half + 2, :]
                nc.vector.tensor_tensor(slot, slot, gate[:, 2 * half:2 * half + 2, :], ALU.add).then_inc(s["last_summed"], 1)


NAMES = ["L0_attn_x", "L0_attn_WQ", "L0_attn_WK", "L0_attn_WV", "L0_ffn_w_gate", "L0_ffn_w1", "L0_ffn_w2", "L0_ffn_w3",
         "L0_ffn_sw1", "L0_ffn_sw2", "L0_ffn_sw3", "L0_ffn_expert_bias"]


def kernel(**inputs):
    import numpy as np
    import concourse.bacc as bacc
    from concourse.bass_utils import run_bass_kernel_spmd

    nc = bacc.Bacc("TRN2", target_bir_lowering=False, num_devices=1)
    arrays, args = {}, []
    for name in NAMES:
        a = np.ascontiguousarray(inputs[name])
        arrays[f"in_{name}"] = a
        args.append(nc.dram_tensor(f"in_{name}", a.shape, mybir.dt.from_np(a.dtype), kind="ExternalInput").ap())
    out = nc.dram_tensor("out", inputs["L0_attn_x"].shape, F32, kind="ExternalOutput").ap()
    build(nc, *args, out)
    r = run_bass_kernel_spmd(nc, [arrays], core_ids=[0])
    return r.results[0]["out"]
```

```python
from contextlib import ExitStack

import concourse.bass as bass
import concourse.mybir as mybir

F32 = mybir.dt.float32
F32R = mybir.dt.float32r
BF16 = mybir.dt.bfloat16
ALU = mybir.AluOpType
ACT = mybir.ActivationFunctionType
AX = mybir.AxisListType

P = 128
EPS = 1e-5
MASKED = -3.0e38
DROPPED = 1.0e38


def build(nc, x, WQ, WK, WV, w_gate, w1, w2, w3, sw1, sw2, sw3, expert_bias, out):
    B, S, D = x.shape
    E, _, H = w1.shape
    T = S // P
    C = D // P
    NT = B * T
    NTOK = B * S
    VG = D + E
    K = 2
    NR = NT * K
    RB = NR // B
    RG = RB // 2
    PAIRS = E * E
    G = 4
    assert S == 512 and D == 256 and H == P and E == 8 and PAIRS == 64 and RG == 4

    with ExitStack() as ctx:
        def sb(name, shape, dt=F32):
            return ctx.enter_context(nc.sbuf_tensor(name, shape, dt))

        def sem(name):
            return ctx.enter_context(nc.semaphore(name))

        bank = [ctx.enter_context(nc.psum_tensor(f"bank{i}", [P, 512], F32)) for i in range(8)]

        xT_hi_all = sb("xT_hi_all", [P, B, C, S], F32R)
        xT_lo_all = sb("xT_lo_all", [P, B, C, S], F32R)
        attn_all = sb("attn_all", [P, NT, D])
        logits = sb("logits", [P, NT, E])

        ident = sb("ident", [P, P])
        ident_bf = sb("ident_bf", [P, P], BF16)
        causal_bf = sb("causal_bf", [P, P], BF16)
        zero_bf = sb("zero_bf", [P, D], BF16)
        ones_bf = sb("ones_bf", [P, P], BF16)
        before = sb("before", [P, G, G])
        neg_half = sb("neg_half", [P, T])
        eps = sb("eps", [P, T])
        iota_e = sb("iota_e", [P, E])
        iota_em = sb("iota_em", [P, E])
        iota_pair = sb("iota_pair", [P, PAIRS])
        row_id = sb("row_id", [P, NT, K])
        partition = sb("partition", [P, 1])
        upper = sb("upper", [P, 1])
        pair_of_partition = sb("pair_of_partition", [P, 1])
        bias_bc = sb("bias_bc", [P, E])

        raw_qkv = sb("raw_qkv", [P, 3, C, D])
        raw_sw = sb("raw_sw", [P, 3, C, D])
        raw_gate = sb("raw_gate", [E, D])
        w13 = sb("w13", [P, 2, E, C, H])
        w2_sb = sb("w2_sb", [P, E, D])
        M_hi = sb("M_hi", [P, C, D], F32R)
        M_lo = sb("M_lo", [P, C, D], F32R)
        WVG_hi = sb("WVG_hi", [P, C, VG], F32R)
        WVG_lo = sb("WVG_lo", [P, C, VG], F32R)

        x_ring = sb("x_ring", [P, 2, T, D])
        xn = sb("xn", [P, T, D])
        probs = sb("probs", [P, 2, S])
        wqT = probs[:, 0, :].rearrange("p (c d) -> p c d", c=C)
        wkT = probs[:, 1, :].rearrange("p (c d) -> p c d", c=C)
        bn = sb("bn", [P, T, 6])
        mv = sb("mv", [P, T, 2])
        var_eps = sb("var_eps", [P, T])
        rstd = sb("rstd", [P, T])
        neg_max = sb("neg_max", [P, T])
        row_sum = sb("row_sum", [P, T])
        row_inv = sb("row_inv", [P, T])

        XT, VV, QT, PT = 2 * C * S, 2 * 2 * T * VG, 2 * C * S, 2 * 2 * S
        arena = sb("arena", [P, XT + VV + QT + PT], F32R)
        xT = arena[:, 0:XT].rearrange("p (h c s) -> p h c s", h=2, c=C)
        v_ring = arena[:, XT:XT + VV].rearrange("p (r h t d) -> p r h t d", r=2, h=2, t=T)
        qT = arena[:, XT + VV:XT + VV + QT].rearrange("p (h c s) -> p h c s", h=2, c=C)
        pT = arena[:, XT + VV + QT:].rearrange("p (r h s) -> p r h s", r=2, h=2)

        SW, HT, SS, OH, PO = 2 * 3 * C * D, 2 * C * S, 2 * RG * 2 * H, RG * P, 2 * RG * PAIRS
        assert SW + HT + SS + 2 * OH + PO + P <= XT + VV + QT + PT
        part_end = [0]

        def part(n):
            part_end[0] += n
            return arena[:, part_end[0] - n:part_end[0]]

        swT = part(SW).rearrange("p (h w c d) -> p h w c d", h=2, w=3, c=C)
        A_stack = part(P)
        assert part_end[0] <= XT + VV // 2
        hT = part(HT).rearrange("p (h c s) -> p h c s", h=2, c=C)
        silu_split = part(SS).rearrange("p (g r h d) -> p g r h d", g=2, r=RG, h=2)
        one_hot_T = part(2 * OH).rearrange("p (g s) -> p g s", g=2)
        pair_one_hot = part(PO).rearrange("p (g r s) -> p g r s", g=2, r=RG)
        A_T = sb("A_T", [P, P], F32R)
        B_T = sb("B_T", [P, PAIRS])
        xn8 = sb("xn8", [P, C, 8])
        w13_flat = w13[:, :, :, :, :].rearrange("p a e c h -> p (a e c h)")
        h_silu = w13_flat[:, 0:C * S].rearrange("p (c s) -> p c s", c=C)
        h_full = w13_flat[:, C * S:2 * C * S].rearrange("p (c s) -> p c s", c=C)
        gate = w13_flat[:, 2 * C * S:3 * C * S].rearrange("p (t d) -> p t d", t=T)
        row_silu = w13_flat[:, 3 * C * S:4 * C * S].rearrange("p (g r d) -> p g r d", g=2, r=RG)
        w_rows = sb("w_rows", [P, NR])
        pair_rows = sb("pair_rows", [P, NR], BF16)

        gs = sb("gs", [P, NT, G])
        l_max = sb("l_max", [P, NT])
        l_sum = sb("l_sum", [P, NT])
        l_inv = sb("l_inv", [P, NT])
        raw_flat = raw_qkv[:, :, :, :].rearrange("p n c d -> p (n c d)")
        RT = NT * E
        ra, rb, rc, rs = [raw_flat[:, n * RT:(n + 1) * RT].rearrange("p (t e) -> p t e", e=E) for n in range(4)]
        scratch_end = [4 * RT]

        def scratch(n):
            scratch_end[0] += n
            return raw_flat[:, scratch_end[0] - n:scratch_end[0]]

        beats = scratch(T * G * 2 * G).rearrange("p (t g u h) -> p t g u h", t=T, g=G, u=2)
        rank = scratch(T * G).rearrange("p (t g) -> p t g", t=T)
        left = scratch(T * E).rearrange("p (t e) -> p t e", t=T)
        best = scratch(T * E).rearrange("p (t e) -> p t e", t=T)
        picked = scratch(T * K * E).rearrange("p (t k e) -> p t k e", t=T, k=K)
        w_picked = scratch(T * K * E).rearrange("p (t k e) -> p t k e", t=T, k=K)
        largest = scratch(T)
        e_of = sb("e_of", [P, NT, K])
        at_least = sb("at_least", [P, NT, K, E], BF16)
        ends = sb("ends", [P, E])
        at_or_past = raw_flat[:, 0:NR * (E - 1)].rearrange("p (r e) -> p r e", e=E - 1)
        g_of = raw_flat[:, 2 * RT:2 * RT + NR]

        sum_w, pair_out = raw_flat[:, 0:H], raw_flat[:, H:H + PAIRS]

        names = """x0_half0 x0_half1 w_loaded x_loaded out_stored last_stored experts_loaded
            const_part const_ready wq_turned wq_ready wk_ready m_summed m_hi_ready m_ready wvg_hi wvg_ready gate_turned
            stats_part stats_done rstd_part rstd_done centered xn0_tiles xn_done x_turned x_hi x_lo xT_copied
            v_summed v_hi v_lo logits_kept q_summed q_hi q_lo scores_done max_done exp_done
            p_turned pT_hi pT_lo pv_done inv_done attn_kept
            sw_turned sw_hi sw_ready xn8_ready tables_summed b_kept a_split a_turned a_ready
            route logits_max shifted route_exp inv_sum scored counted rows_ready
            h1_done h3_done h_silu_done h_mult_done h_hi h_lo o_done gate_done gated summed
            bc_done one_hot_done gathered rows_silu rows_hi rows_lo pair_one_hot_done accumulated0 accumulated1
            inv_part wqk_loaded sum_ready sum_turned pairs_ready last_tile_done last_gate_done last_gated last_summed bias_loaded""".split()
        s = {n: sem(n) for n in names}

        x_v = x.rearrange("b (t p) d -> b p t d", p=P)
        out_v = out.rearrange("b (t p) d -> b p t d", p=P)
        block = ctx.enter_context(nc.Block())

        LOOP1 = B - 2
        LAST_PIECES = (slice(0, 2), slice(2, 3), slice(3, 4))
        WARM_UP = 18
        ROUTE = 20
        ROUTED = 2 + ROUTE * B

        def sequence(i):
            return 0 if isinstance(i, int) and i == B - 1 else i + 1

        @block.sync
        def _(sp):
            def load_x(b, slot_b):
                sp.dma_start(x_ring[:, slot_b % 2, :, :], x_v[b, :, :, :]).then_inc(s["x_loaded"], 16)

            for half in range(2):
                t2 = slice(2 * half, 2 * half + 2)
                sp.dma_start(x_ring[:, 0, t2, :], x_v[0, :, t2, :]).then_inc(s[f"x0_half{half}"], 16)
            for n, w in enumerate((WQ, WK)):
                sp.dma_start(raw_qkv[:, n, :, :], w.rearrange("(c p) k -> p c k", p=P)).then_inc(s["wqk_loaded"], 16)
            sp.dma_start(raw_qkv[:, 2, :, :], WV.rearrange("(c p) k -> p c k", p=P)).then_inc(s["w_loaded"], 16)
            sp.dma_start(raw_gate[:, :], w_gate).then_inc(s["w_loaded"], 16)
            sp.dma_start(bias_bc[:, :], expert_bias.unsqueeze(0).to_broadcast([P, E])).then_inc(s["bias_loaded"], 16)
            load_x(1, 1)

            def copy_xT(b):
                sp.wait_ge(s["x_lo"], C * (b + 1))
                for h, dst in enumerate((xT_hi_all, xT_lo_all)):
                    sp.dma_start(dst[:, b, :, :].bitcast(F32), xT[:, h, :, :].bitcast(F32)).then_inc(s["xT_copied"], 16)

            def step(b):
                sp.wait_ge(s["xn_done"], b + 1)
                sp.wait_ge(s["x_loaded"], 16 * b + 16)
                load_x(b + 2, b)
                copy_xT(b)

            step(0)
            for n, w in enumerate((sw1, sw3, sw2)):
                sp.dma_start(raw_sw[:, n, :, :], w.rearrange("(c p) k -> p c k", p=P)).then_inc(s["experts_loaded"], 16)
            for n, w in enumerate((w1, w3)):
                sp.dma_start(w13[:, n, :, :, :], w.rearrange("e (c p) h -> p e c h", p=P)).then_inc(s["experts_loaded"], 16)
            sp.dma_start(w2_sb[:, :, :], w2.rearrange("e h d -> h e d")).then_inc(s["experts_loaded"], 16)
            with sp.Fori(1, LOOP1) as b:
                step(b)
            copy_xT(B - 2)
            copy_xT(B - 1)

            def reload_x(i):
                sp.wait_ge(s["x_loaded"], 16 * (B + i - 1))
                load_x(sequence(i), i)

            sp.wait_ge(s["xn_done"], B)
            reload_x(0)
            reload_x(1)

            def store(i):
                sp.wait_ge(s["summed"], i + 1)
                sp.dma_start(out_v[sequence(i), :, :, :], x_ring[:, i % 2, :, :]).then_inc(s["out_stored"], 16)
                sp.wait_ge(s["out_stored"], 16 * (i + 1))

            with sp.Fori(0, B - 3) as i:
                store(i)
                reload_x(i + 2)
            store(B - 3)
            reload_x(B - 1)
            store(B - 2)
            for n in (1, 0, 2):
                tiles = LAST_PIECES[n]
                if n == 0:
                    sp.wait_ge(s["summed"], B)
                else:
                    sp.wait_ge(s["last_summed"], n)
                sp.dma_start(out_v[0, :, tiles, :], x_ring[:, (B - 1) % 2, tiles, :]).then_inc(s["last_stored"], 16)
            sp.wait_ge(s["last_stored"], 16 * len(LAST_PIECES))

        @block.gpsimd
        def _(pool):
            def made(ins):
                ins.then_inc(s["const_part"], 1)

            made(nc.gpsimd.memset(ident[:, :], 0.0))
            made(nc.gpsimd.memset(causal_bf[:, :], 0.0))
            made(nc.gpsimd.memset(before[:, :, :], 1.0))
            made(nc.gpsimd.memset(neg_half[:, :], -0.5))
            made(nc.gpsimd.memset(eps[:, :], EPS))
            made(nc.gpsimd.memset(zero_bf[:, :], 0.0))
            made(nc.gpsimd.memset(ones_bf[:, :], 1.0))
            pool.wait_ge(s["const_part"], 7)
            made(nc.gpsimd.affine_select(out=ident[:, :], in_=ident[:, :], compare_op=ALU.not_equal, fill=1.0, base=0,
                                         pattern=[[-1, P]], channel_multiplier=1))
            made(nc.gpsimd.affine_select(out=causal_bf[:, :], in_=causal_bf[:, :], compare_op=ALU.is_ge, fill=MASKED,
                                         base=0, pattern=[[-1, P]], channel_multiplier=1))
            made(nc.gpsimd.affine_select(out=before[:, :, :], in_=before[:, :, :], compare_op=ALU.is_ge, fill=0.0, base=-1,
                                         pattern=[[1, G], [-1, G]], channel_multiplier=0))
            pool.wait_ge(s["const_part"], 10)
            nc.gpsimd.tensor_copy(ident_bf[:, :], ident[:, :]).then_inc(s["const_ready"], 1)

            def rstd_of(b):
                pool.wait_ge(s["stats_done"], b + 1)
                nc.gpsimd.tensor_tensor(var_eps[:, :], mv[:, :, 1], eps[:, :], ALU.add).then_inc(s["rstd_part"], 1)
                pool.wait_ge(s["rstd_part"], b + 1)
                if not isinstance(b, int) or b > 0:
                    pool.wait_ge(s["xn_done"], b)
                nc.gpsimd.tensor_tensor(rstd[:, :], var_eps[:, :], neg_half[:, :], ALU.pow).then_inc(s["rstd_done"], 1)

            def normalise(n, half):
                t2 = slice(2 * half, 2 * half + 2)
                if half == 0:
                    pool.wait_ge(s["x_turned"], C * n)
                nc.gpsimd.tensor_tensor(xn[:, t2, :], x_ring[:, n % 2, t2, :], mv[:, t2, 0:1].to_broadcast([P, 2, D]),
                                        ALU.subtract).then_inc(s["centered"], 1)
                pool.wait_ge(s["centered"], 2 * n - 3 + half)
                ins = nc.gpsimd.tensor_tensor(xn[:, t2, :], xn[:, t2, :], rstd[:, t2].unsqueeze(2).to_broadcast([P, 2, D]),
                                              ALU.mult)
                if half == 1:
                    ins.then_inc(s["xn_done"], 1)

            def iota(dst, pattern, base, mult):
                nc.gpsimd.iota(dst, pattern=pattern, base=base, channel_multiplier=mult,
                               allow_small_or_imprecise_dtypes=True).then_inc(s["const_ready"], 1)

            rstd_of(0)
            iota(iota_e[:, :], [[1, E]], 0, 0)
            iota(iota_em[:, :], [[1, E]], -8, 0)
            iota(iota_pair[:, :], [[1, PAIRS]], -8, 0)
            iota(row_id[:, :, :], [[K * P, NT], [1, K]], 0, K)
            iota(partition[:, :], [[0, 1]], -8, 1)

            def keep_logits(b):
                pool.wait_ge(s["v_lo"], T * (b + 1))
                nc.gpsimd.tensor_tensor(logits[:, bass.ds(b * T, T), :], v_ring[:, b % 2, 0, :, D:VG].bitcast(F32),
                                        v_ring[:, b % 2, 1, :, D:VG].bitcast(F32), ALU.add).then_inc(s["logits_kept"], 1)

            def shift_logits(b):
                tiles = bass.ds(b * T, T)
                pool.wait_ge(s["logits_max"], b + 1)
                nc.gpsimd.tensor_tensor(ra[:, tiles, :], logits[:, tiles, :], l_max[:, tiles].unsqueeze(2).to_broadcast([P, T, E]),
                                        ALU.subtract).then_inc(s["shifted"], 1)

            def score(b):
                tiles = bass.ds(b * T, T)
                pool.wait_ge(s["inv_sum"], b + 1)
                nc.gpsimd.tensor_tensor(rc[:, tiles, :], rb[:, tiles, :], l_inv[:, tiles].unsqueeze(2).to_broadcast([P, T, E]),
                                        ALU.mult).then_inc(s["scored"], 1)
                pool.wait_ge(s["scored"], 3 * b + 1)
                nc.gpsimd.tensor_tensor(rs[:, tiles, :], rc[:, tiles, :], bias_bc[:, :].unsqueeze(1).to_broadcast([P, T, E]),
                                        ALU.add).then_inc(s["scored"], 1)
                pool.wait_ge(s["scored"], 3 * b + 2)
                both = rs[:, tiles, :].rearrange("p t (g u) -> p t g u", u=2)
                nc.gpsimd.tensor_tensor(gs[:, tiles, :], both[:, :, :, 0], both[:, :, :, 1], ALU.add).then_inc(s["scored"], 1)

            rstd_of(1)
            keep_logits(0)
            pool.wait_ge(s["bias_loaded"], 16)
            with pool.Fori(0, LOOP1) as b:
                shift_logits(b)
                rstd_of(b + 2)
                normalise(b + 2, 0)
                normalise(b + 2, 1)
                score(b)
                keep_logits(b + 1)
            shift_logits(B - 2)
            score(B - 2)
            keep_logits(B - 1)
            shift_logits(B - 1)
            score(B - 1)

            def add_x(i):
                pool.wait_ge(s["x_loaded"], 16 * (B + i))
                pool.wait_ge(s["gated"], 2 * (i + 1))
                slot = x_ring[:, i % 2, :, :]
                nc.gpsimd.tensor_tensor(slot, slot, gate[:, :, :], ALU.add).then_inc(s["summed"], 1)

            with pool.Fori(0, B - 1) as i:
                add_x(i)
            pool.wait_ge(s["x_loaded"], 16 * (2 * B - 1))
            pool.wait_ge(s["last_gated"], 1)
            slot = x_ring[:, (B - 1) % 2, LAST_PIECES[0], :]
            nc.gpsimd.tensor_tensor(slot, slot, gate[:, LAST_PIECES[0], :], ALU.add).then_inc(s["summed"], 1)

        @block.tensor
        def _(pe):
            def mm(dst, lhsT, rhs, start, stop, **kw):
                return nc.tensor.matmul(dst, lhsT, rhs, start=start, stop=stop, skip_group_check=True, **kw)

            def split_products(dst, terms, onto=False):
                last = len(terms) - 1
                for n, (lh, ll, rh, rl) in enumerate(terms):
                    mm(dst, lh, rh, n == 0 and not onto, False)
                    mm(dst, lh, rl, False, False)
                    ins = mm(dst, ll, rh, False, n == last)
                return ins

            pe.wait_ge(s["const_part"], 7)
            for _ in range(WARM_UP):
                mm(bank[7][:, 0:D], zero_bf[:, 0:P], zero_bf[:, :], True, True)

            pe.wait_ge(s["const_ready"], 1)
            pe.wait_ge(s["wqk_loaded"], 16 * 2)
            for n in range(2):
                for kc in range(C):
                    for dc in range(C):
                        ins = nc.tensor.transpose(bank[n][:, kc * D + dc * P:kc * D + (dc + 1) * P],
                                                  raw_qkv[:, n, dc, kc * P:(kc + 1) * P], ident[:, :])
                ins.then_inc(s["wq_turned"], 1)
            pe.wait_ge(s["w_loaded"], 16 * 2)
            for dc in range(C):
                ins = nc.tensor.transpose(bank[2][:, dc * E:(dc + 1) * E], raw_gate[:, dc * P:(dc + 1) * P], ident[0:E, 0:E])
            ins.then_inc(s["gate_turned"], 1)
            sc_bank, pt_bank, pv_bank, v_bank, x_bank = bank[0:2], bank[2:4], bank[4], bank[5], bank[6:8]
            first_v_banks = [bank[5], bank[4], bank[2], bank[3]]

            def turn_x0():
                for t in range(T):
                    if t < T - 1:
                        pe.wait_ge(s["xn0_tiles"], t + 1)
                    else:
                        pe.wait_ge(s["xn_done"], 1)
                    for c in range(C):
                        ins = nc.tensor.transpose(x_bank[c][:, t * P:(t + 1) * P], xn[:, t, c * P:(c + 1) * P], ident[:, :])
                        if t == T - 1:
                            ins.then_inc(s["x_turned"], 1)

            def turn_x(b, c):
                pe.wait_ge(s["xn_done"], b + 1)
                if not isinstance(b, int) or b > 0:
                    pe.wait_ge(s["q_lo"], C * b)
                for t in range(T):
                    ins = nc.tensor.transpose(x_bank[c][:, t * P:(t + 1) * P], xn[:, t, c * P:(c + 1) * P], ident[:, :])
                ins.then_inc(s["x_turned"], 1)

            def values(b, t):
                tok = slice(t * P, (t + 1) * P)
                dst = v_bank
                if isinstance(b, int) and b == 0:
                    dst = first_v_banks[t]
                else:
                    pe.wait_ge(s["v_lo"], T * b + t)
                if t == 0:
                    pe.wait_ge(s["x_lo"], C * (b + 1))
                split_products(dst[:, 0:VG], [(xT[:, 0, c, tok], xT[:, 1, c, tok], WVG_hi[:, c, :], WVG_lo[:, c, :])
                                              for c in range(C)]).then_inc(s["v_summed"], 1)

            def queries(b, ec):
                pe.wait_ge(s["x_lo"], C * (b + 1))
                e = slice(ec * P, (ec + 1) * P)
                split_products(x_bank[ec][:, :], [(M_hi[:, c, e], M_lo[:, c, e], xT[:, 0, c, :], xT[:, 1, c, :])
                                                  for c in range(C)]).then_inc(s["q_summed"], 1)

            def scores(b, i):
                if i == 0:
                    pe.wait_ge(s["q_lo"], C * (b + 1))
                    pe.wait_ge(s["xT_copied"], 32 * (b + 1))
                if i >= 2 or not isinstance(b, int) or b > 0:
                    pe.wait_ge(s["exp_done"], T * b + i - 1)
                n = (i + 1) * P
                tok = slice(i * P, n)
                dst = sc_bank[i % 2][:, 0:n]
                split_products(dst, [(qT[:, 0, c, tok], qT[:, 1, c, tok], xT_hi_all[:, b, c, 0:n], xT_lo_all[:, b, c, 0:n])
                                     for c in range(C)])
                mm(sc_bank[i % 2][:, i * P:n], ident_bf[:, :], causal_bf[:, :], False, True).then_inc(s["scores_done"], 1)

            def turn_probs(b, i):
                pe.wait_ge(s["exp_done"], T * b + i + 1)
                if i >= 2 or not isinstance(b, int) or b > 0:
                    pe.wait_ge(s["pT_lo"], T * b + i - 1)
                for j in range(i + 1):
                    ins = nc.tensor.transpose(pt_bank[i % 2][:, j * P:(j + 1) * P], probs[:, i % 2, j * P:(j + 1) * P], ident[:, :])
                ins.then_inc(s["p_turned"], 1)

            def weigh(b, i):
                pe.wait_ge(s["pT_lo"], T * b + i + 1)
                if i > 0 or not isinstance(b, int) or b > 0:
                    pe.wait_ge(s["attn_kept"], T * b + i)
                split_products(pv_bank[:, 0:D], [(pT[:, i % 2, 0, j * P:(j + 1) * P], pT[:, i % 2, 1, j * P:(j + 1) * P],
                                                  v_ring[:, b % 2, 0, j, 0:D], v_ring[:, b % 2, 1, j, 0:D])
                                                 for j in range(i + 1)]).then_inc(s["pv_done"], 1)

            turn_x0()
            pe.wait_ge(s["wq_ready"], 1)
            pe.wait_ge(s["wk_ready"], 1)
            for dc in range(C):
                for kc in range(C):
                    ins = mm(bank[3][:, dc * D:(dc + 1) * D], wqT[:, kc, dc * P:(dc + 1) * P], wkT[:, kc, :],
                             kc == 0, kc == C - 1)
            ins.then_inc(s["m_summed"], 1)

            pe.wait_ge(s["wvg_ready"], 1)
            values(0, 0)
            values(0, 1)
            pe.wait_ge(s["m_ready"], 1)
            queries(0, 0)
            queries(0, 1)
            values(0, 2)
            values(0, 3)

            def step(b):
                p = b + 1
                scores(b, 0)
                turn_x(p, 0)
                scores(b, 1)
                turn_x(p, 1)
                turn_probs(b, 0)
                scores(b, 2)
                scores(b, 3)
                turn_probs(b, 1)
                values(p, 0)
                weigh(b, 0)
                queries(p, 0)
                turn_probs(b, 2)
                values(p, 1)
                queries(p, 1)
                weigh(b, 1)
                values(p, 2)
                turn_probs(b, 3)
                weigh(b, 2)
                values(p, 3)
                weigh(b, 3)

            step(0)
            with pe.Fori(1, LOOP1) as b:
                step(b)
            step(B - 2)

            b = B - 1
            sw_bank = [x_bank[0], x_bank[1], v_bank]

            def turn_sw(n):
                if n == 0:
                    pe.wait_ge(s["experts_loaded"], 16 * 6)
                pe.wait_ge(*((s["q_lo"], C * B) if n < 2 else (s["v_lo"], T * B)))
                for kc in range(C):
                    for dc in range(C):
                        ins = nc.tensor.transpose(sw_bank[n][:, kc * D + dc * P:kc * D + (dc + 1) * P],
                                                  raw_sw[:, n, dc, kc * P:(kc + 1) * P], ident[:, :])
                ins.then_inc(s["sw_turned"], 1)

            table_bank = [x_bank[0], x_bank[1]]

            def table(n, quarter):
                pe.wait_ge(s["xn8_ready"], 1)
                pe.wait_ge(s["sw_ready"], 1 + n)
                for g in range(quarter * E // 4, (quarter + 1) * E // 4):
                    for c in range(C):
                        ins = mm(table_bank[n][:, g * 8:(g + 1) * 8], w13[:, n, g, c, :], xn8[:, c, :],
                                 c == 0, c == C - 1)
                ins.then_inc(s["tables_summed"], 1)

            scores(b, 0)
            scores(b, 1)
            turn_sw(0)
            turn_probs(b, 0)
            scores(b, 2)
            turn_sw(1)
            turn_probs(b, 1)
            scores(b, 3)
            turn_sw(2)
            table(0, 0)
            weigh(b, 0)
            turn_probs(b, 2)
            table(0, 1)
            weigh(b, 1)
            turn_probs(b, 3)
            table(0, 2)
            weigh(b, 2)
            table(0, 3)
            weigh(b, 3)

            h1_bank, h3_bank, o_bank, bc_bank, g_bank, acc_bank = bank[0:2], bank[2:4], bank[4], bank[5], bank[6], bank[7]

            def hidden(i, hc, w, dst, done):
                b = sequence(i)
                if not isinstance(i, int) or i > 0:
                    pe.wait_ge(s["h_mult_done"], C * i + hc - (C - 1))
                hid = slice(hc * P, (hc + 1) * P)
                split_products(dst[hc][:, :], [(swT[:, 0, w, c, hid], swT[:, 1, w, c, hid], xT_hi_all[:, b, c, :], xT_lo_all[:, b, c, :])
                                               for c in range(C)]).then_inc(s[done], 1)

            def routed_out():
                mm(o_bank[:, 0:D], zero_bf[:, 0:P], zero_bf[:, :], True, False)
                pe.wait_ge(s["pairs_ready"], 1)
                for g in range(E):
                    mm(o_bank[0:8, 0:D], pair_out[:, g * 8:(g + 1) * 8], w2_sb[:, g, :], False, False)

            def out_tile(t, dst, onto=False):
                tok = slice(t * P, (t + 1) * P)
                return split_products(dst, [(hT[:, 0, c, tok], hT[:, 1, c, tok], swT[:, 0, 2, c, :], swT[:, 1, 2, c, :])
                                            for c in range(C)], onto=onto)

            def shared_out(i, half):
                if half == 0:
                    pe.wait_ge(s["h_lo"], C * (i + 1))
                if half == 1 or not isinstance(i, int) or 0 < i < B - 1:
                    pe.wait_ge(s["gate_done"], 2 * i + half)
                for u in range(2):
                    ins = out_tile(2 * half + u, o_bank[:, u * D:(u + 1) * D], onto=isinstance(i, int) and i == B - 1 and u == 0)
                ins.then_inc(s["o_done"], 1)

            def spread_pairs(i, g):
                if g == 1 or not isinstance(i, int) or i > 0:
                    pe.wait_ge(s["one_hot_done"], 2 * i + g)
                for j in range(RG):
                    r = g * RG + j
                    ins = mm(bc_bank[:, j * P:(j + 1) * P], pair_rows[:, bass.ds(i * RB + r, 1)].to_broadcast([P, P]), ident_bf[:, :], True, True)
                ins.then_inc(s["bc_done"], 1)

            def gather(i, g):
                pe.wait_ge(s["one_hot_done"], 2 * i + g + 1)
                if g == 1 or not isinstance(i, int) or i > 0:
                    pe.wait_ge(s["rows_silu"], RB * i + RG * g)
                for j in range(RG):
                    ins = mm(g_bank[:, j * H:(j + 1) * H], one_hot_T[:, g, j * P:(j + 1) * P], A_stack, True, True)
                ins.then_inc(s["gathered"], 1)

            def accumulate(i, g):
                pe.wait_ge(s["rows_lo"], 2 * i + g + 1)
                pe.wait_ge(s["pair_one_hot_done"], 2 * i + g + 1)
                for j in range(RG):
                    ins = mm(acc_bank[0:PAIRS, 0:2 * H], pair_one_hot[:, g, j, :],
                             silu_split[:, g, j, :, :].rearrange("p h d -> p (h d)"), False, True)
                ins.then_inc(s[f"accumulated{g}"], 1)

            pe.wait_ge(s["a_split"], 2)
            nc.tensor.transpose(x_bank[0][:, 0:P], A_T[:, :].bitcast(F32), ident[:, :]).then_inc(s["a_turned"], 1)
            table(1, 0)
            pe.wait_ge(s["sw_ready"], 3)
            pe.wait_ge(s["exp_done"], T * B)
            hidden(0, 0, 0, h1_bank, "h1_done")
            table(1, 1)
            pe.wait_ge(s["route"], ROUTED)
            for n in range(4):
                ins = mm(bc_bank[:, 0:P], ones_bf[:, :], at_least[:, :, :, :].rearrange("p t k e -> p (t k e)")[:, n * P:(n + 1) * P],
                         n == 0, n == 3)
            ins.then_inc(s["counted"], 1)
            pe.wait_ge(s["pT_lo"], T * B)
            hidden(0, 0, 1, h3_bank, "h3_done")
            table(1, 2)
            pe.wait_ge(s["rows_ready"], 1)
            spread_pairs(0, 0)
            hidden(0, 1, 0, h1_bank, "h1_done")
            pe.wait_ge(s["a_ready"], 1)
            gather(0, 0)
            spread_pairs(0, 1)
            table(1, 3)
            hidden(0, 1, 1, h3_bank, "h3_done")
            gather(0, 1)
            pe.wait_ge(s["attn_kept"], T * B)
            pe.wait_ge(s["b_kept"], 1)
            mm(acc_bank[0:PAIRS, 0:2 * H], zero_bf[:, 0:PAIRS], zero_bf[:, 0:2 * H], True, True)

            def step2(i):
                hidden(i, 0, 0, h1_bank, "h1_done")
                hidden(i, 0, 1, h3_bank, "h3_done")
                spread_pairs(i, 0)
                shared_out(i - 1, 0)
                accumulate(i - 1, 0)
                gather(i, 0)
                spread_pairs(i, 1)
                hidden(i, 1, 0, h1_bank, "h1_done")
                shared_out(i - 1, 1)
                gather(i, 1)
                hidden(i, 1, 1, h3_bank, "h3_done")
                accumulate(i - 1, 1)

            with pe.Fori(1, B - 1) as i:
                step2(i)
            i = B - 1
            spread_pairs(i, 0)
            accumulate(i - 1, 0)
            hidden(i, 0, 0, h1_bank, "h1_done")
            hidden(i, 0, 1, h3_bank, "h3_done")
            gather(i, 0)
            spread_pairs(i, 1)
            shared_out(i - 1, 0)
            accumulate(i - 1, 1)
            gather(i, 1)
            hidden(i, 1, 0, h1_bank, "h1_done")
            hidden(i, 1, 1, h3_bank, "h3_done")
            accumulate(i, 0)
            shared_out(i - 1, 1)
            accumulate(i, 1)
            pe.wait_ge(s["sum_ready"], 1)
            nc.tensor.transpose(bc_bank[:, 0:PAIRS], sum_w[0:PAIRS, :], ident[0:PAIRS, 0:PAIRS]).then_inc(s["sum_turned"], 1)
            pe.wait_ge(s["gate_done"], 2 * i)
            routed_out()
            shared_out(i, 0)
            pe.wait_ge(s["rows_silu"], RB * B)
            for t, dst in ((2, g_bank), (3, bc_bank)):
                out_tile(t, dst[:, 0:D]).then_inc(s["last_tile_done"], 1)

        @block.scalar
        def _(act):
            sc_bank, pt_bank, pv_bank, v_bank, x_bank = bank[0:2], bank[2:4], bank[4], bank[5], bank[6:8]
            first_v_banks = [bank[5], bank[4], bank[2], bank[3]]

            def copy(dst, src, scale=1.0):
                return nc.scalar.activation(dst, src, ACT.Copy, scale=scale)

            def x_high(b, c):
                if not isinstance(b, int) or b > 0:
                    act.wait_ge(s["xT_copied"], 32 * b)
                    act.wait_ge(s["v_summed"], T * b)
                    act.wait_ge(s["q_summed"], C * b)
                act.wait_ge(s["x_turned"], C * b + c + 1)
                copy(xT[:, 0, c, :], x_bank[c][:, :]).then_inc(s["x_hi"], 1)

            def v_high(b, t):
                src = first_v_banks[t] if isinstance(b, int) and b == 0 else v_bank
                act.wait_ge(s["v_summed"], T * b + t + 1)
                copy(v_ring[:, b % 2, 0, t, :], src[:, 0:VG]).then_inc(s["v_hi"], 1)

            def q_high(b, c):
                act.wait_ge(s["q_summed"], C * b + c + 1)
                if c == 0 and (not isinstance(b, int) or b > 0):
                    act.wait_ge(s["scores_done"], T * b)
                copy(qT[:, 0, c, :], x_bank[c][:, :]).then_inc(s["q_hi"], 1)

            def soft(b, i):
                act.wait_ge(s["max_done"], T * b + i + 1)
                if i >= 2 or not isinstance(b, int) or b > 0:
                    act.wait_ge(s["p_turned"], T * b + i - 1)
                if not isinstance(b, int) or b > 0:
                    act.wait_ge(s["inv_done"], T * b + i + 1 - T)
                n = (i + 1) * P
                nc.scalar.activation(probs[:, i % 2, 0:n], sc_bank[i % 2][:, 0:n], ACT.Exp, bias=neg_max[:, i:i + 1],
                                     accum_out=row_sum[:, i:i + 1]).then_inc(s["exp_done"], 1)

            def p_high(b, i):
                act.wait_ge(s["p_turned"], T * b + i + 1)
                if i >= 2 or not isinstance(b, int) or b > 0:
                    act.wait_ge(s["pv_done"], T * b + i - 1)
                n = (i + 1) * P
                copy(pT[:, i % 2, 0, 0:n], pt_bank[i % 2][:, 0:n]).then_inc(s["pT_hi"], 1)

            def keep_attn(b, i):
                act.wait_ge(s["pv_done"], T * b + i + 1)
                act.wait_ge(s["inv_done"], T * b + i + 1)
                copy(attn_all[:, b * T + i, :], pv_bank[:, 0:D], scale=row_inv[:, i:i + 1]).then_inc(s["attn_kept"], 1)

            def exp_logits(b):
                tiles = bass.ds(b * T, T)
                act.wait_ge(s["shifted"], b + 1)
                nc.scalar.activation(rb[:, tiles, :], ra[:, tiles, :], ACT.Exp).then_inc(s["route_exp"], 1)

            act.wait_ge(s["w_loaded"], 16 * 2)
            copy(WVG_hi[:, :, 0:D], raw_qkv[:, 2, :, :]).then_inc(s["wvg_hi"], 1)
            act.wait_ge(s["wq_turned"], 1)
            copy(probs[:, 0, :], bank[0][:, :]).then_inc(s["wq_ready"], 1)
            act.wait_ge(s["wq_turned"], 2)
            copy(probs[:, 1, :], bank[1][:, :]).then_inc(s["wk_ready"], 1)
            act.wait_ge(s["gate_turned"], 1)
            copy(WVG_hi[:, :, D:VG], bank[2][:, 0:C * E].rearrange("p (c e) -> p c e", c=C)).then_inc(s["wvg_hi"], 1)
            x_high(0, 0)
            x_high(0, 1)
            act.wait_ge(s["m_summed"], 1)
            copy(M_hi[:, :, :].rearrange("p c d -> p (c d)"), bank[3][:, :], scale=D ** -0.5).then_inc(s["m_hi_ready"], 1)
            v_high(0, 0)
            v_high(0, 1)
            q_high(0, 0)
            q_high(0, 1)
            v_high(0, 2)
            v_high(0, 3)

            def step(b):
                p = b + 1
                soft(b, 0)
                x_high(p, 0)
                soft(b, 1)
                p_high(b, 0)
                x_high(p, 1)
                exp_logits(b)
                v_high(p, 0)
                p_high(b, 1)
                soft(b, 2)
                keep_attn(b, 0)
                q_high(p, 0)
                v_high(p, 1)
                p_high(b, 2)
                soft(b, 3)
                q_high(p, 1)
                keep_attn(b, 1)
                v_high(p, 2)
                p_high(b, 3)
                keep_attn(b, 2)
                v_high(p, 3)
                keep_attn(b, 3)

            step(0)
            with act.Fori(1, LOOP1) as b:
                step(b)
            step(B - 2)

            b = B - 1
            sw_bank = [x_bank[0], x_bank[1], v_bank]

            def sw_high(n):
                if n == 0:
                    act.wait_ge(s["xT_copied"], 32 * B)
                act.wait_ge(s["sw_turned"], n + 1)
                copy(swT[:, 0, n, :, :].rearrange("p c d -> p (c d)"), sw_bank[n][:, :]).then_inc(s["sw_hi"], 1)

            soft(b, 0)
            soft(b, 1)
            exp_logits(b)
            p_high(b, 0)
            sw_high(0)
            soft(b, 2)
            p_high(b, 1)
            sw_high(1)
            soft(b, 3)
            keep_attn(b, 0)
            p_high(b, 2)
            sw_high(2)
            p_high(b, 3)
            keep_attn(b, 1)
            keep_attn(b, 2)
            act.wait_ge(s["tables_summed"], 4)
            copy(A_T[:, 0:PAIRS], x_bank[0][:, 0:PAIRS]).then_inc(s["a_split"], 1)
            keep_attn(b, 3)
            act.wait_ge(s["a_turned"], 1)
            copy(A_stack, x_bank[0][:, 0:P]).then_inc(s["a_ready"], 1)

            h1_bank, h3_bank, o_bank, bc_bank, g_bank, acc_bank = bank[0:2], bank[2:4], bank[4], bank[5], bank[6], bank[7]

            def silu_hidden(i, hc):
                act.wait_ge(s["h1_done"], C * i + hc + 1)
                if not isinstance(i, int) or i > 0:
                    act.wait_ge(s["h_mult_done"], C * i + hc - (C - 1))
                nc.scalar.activation(h_silu[:, hc, :], h1_bank[hc][:, :], ACT.Silu).then_inc(s["h_silu_done"], 1)

            def h_high(i, hc):
                act.wait_ge(s["h_mult_done"], C * i + hc + 1)
                if not isinstance(i, int) or i > 0:
                    act.wait_ge(s["o_done"], 2 * i)
                copy(hT[:, 0, hc, :], h_full[:, hc, :]).then_inc(s["h_hi"], 1)

            def silu_rows(i, g):
                act.wait_ge(s["route"], ROUTED)
                act.wait_ge(s["gathered"], 2 * i + g + 1)
                if not isinstance(i, int) or i > 0:
                    act.wait_ge(s["rows_lo"], 2 * i + g - 1)
                for j in range(RG):
                    r = g * RG + j
                    nc.scalar.activation(row_silu[:, g, j, :], g_bank[:, j * H:(j + 1) * H], ACT.Silu,
                                         scale=w_rows[:, bass.ds(i * RB + r, 1)]).then_inc(s["rows_silu"], 1)

            def rows_high(i, g):
                act.wait_ge(s["rows_silu"], RB * i + RG * (g + 1))
                if not isinstance(i, int) or i > 0:
                    act.wait_ge(s[f"accumulated{g}"], i)
                for j in range(RG):
                    weight = w_rows[:, :].rearrange("p (t k) -> p t k", k=K)[:, bass.ds(i * T + (g * RG + j) // K, 1), j % K]
                    ins = copy(silu_split[:, g, j, 0, :], row_silu[:, g, j, :], scale=weight)
                ins.then_inc(s["rows_hi"], 1)

            def silu_out(i, half):
                act.wait_ge(s["o_done"], 2 * i + half + 1)
                if not isinstance(i, int) or i > 0:
                    act.wait_ge(s["summed"], i)
                nc.scalar.activation(gate[:, 2 * half:2 * half + 2, :].rearrange("p t d -> p (t d)"), o_bank[:, :],
                                     ACT.Silu).then_inc(s["gate_done"], 1)

            silu_hidden(0, 0)
            h_high(0, 0)
            silu_rows(0, 0)
            silu_hidden(0, 1)
            rows_high(0, 0)
            silu_rows(0, 1)
            h_high(0, 1)
            rows_high(0, 1)

            def step2(i):
                silu_hidden(i, 0)
                silu_out(i - 1, 0)
                silu_rows(i, 0)
                rows_high(i, 0)
                silu_hidden(i, 1)
                silu_rows(i, 1)
                silu_out(i - 1, 1)
                h_high(i, 0)
                h_high(i, 1)
                rows_high(i, 1)

            with act.Fori(1, B - 1) as i:
                step2(i)
            i = B - 1
            silu_hidden(i, 0)
            silu_rows(i, 0)
            rows_high(i, 0)
            silu_rows(i, 1)
            silu_out(i - 1, 0)
            rows_high(i, 1)
            silu_hidden(i, 1)
            silu_out(i - 1, 1)
            h_high(i, 0)
            h_high(i, 1)
            silu_out(i, 0)
            for t, src in ((2, g_bank), (3, bc_bank)):
                act.wait_ge(s["last_tile_done"], t - 1)
                nc.scalar.activation(gate[:, t, :], src[:, 0:D], ACT.Silu).then_inc(s["last_gate_done"], 1)

        @block.vector
        def _(dve):
            sc_bank, pt_bank, pv_bank, v_bank, x_bank = bank[0:2], bank[2:4], bank[4], bank[5], bank[6:8]
            first_v_banks = [bank[5], bank[4], bank[2], bank[3]]

            def low(dst, src, high):
                return nc.vector.tensor_tensor(dst, src, high.bitcast(F32), ALU.subtract)

            def stats(b, t):
                if isinstance(b, int) and b == 0:
                    dve.wait_ge(s[f"x0_half{t // 2}"], 16)
                elif t == 0:
                    dve.wait_ge(s["x_loaded"], 16 * (b + 1) - 16)
                if t == T - 1 and (not isinstance(b, int) or b > 2):
                    dve.wait_ge(s["centered"], 2 * b - 4)
                ins = nc.vector.bn_stats(bn[:, t, :], x_ring[:, b % 2, t, :])
                if t == T - 1:
                    ins.then_inc(s["stats_part"], 1)

            def mean_var(b):
                dve.wait_ge(s["const_ready"], 1)
                dve.wait_ge(s["stats_part"], b + 1)
                if not isinstance(b, int) or b > 0:
                    dve.wait_ge(s["rstd_part"], b)
                for t in range(T):
                    ins = nc.vector.bn_aggr(mv[:, t, :], bn[:, t, :])
                ins.then_inc(s["stats_done"], 1)

            def scale_x(b, t):
                if t == 0:
                    dve.wait_ge(s["rstd_done"], b + 1)
                    if b > 0:
                        dve.wait_ge(s["x_turned"], C * b)
                ins = nc.vector.tensor_scalar(xn[:, t, :], x_ring[:, b, t, :], mv[:, t, 0:1], rstd[:, t:t + 1],
                                              ALU.subtract, ALU.mult)
                if t == T - 1:
                    ins.then_inc(s["xn_done"], 1)
                elif b == 0:
                    ins.then_inc(s["xn0_tiles"], 1)

            def x_low(b, c):
                dve.wait_ge(s["x_hi"], C * b + c + 1)
                low(xT[:, 1, c, :], x_bank[c][:, :], xT[:, 0, c, :]).then_inc(s["x_lo"], 1)

            def v_low(b, t):
                src = first_v_banks[t] if isinstance(b, int) and b == 0 else v_bank
                dve.wait_ge(s["v_hi"], T * b + t + 1)
                low(v_ring[:, b % 2, 1, t, :], src[:, 0:VG], v_ring[:, b % 2, 0, t, :]).then_inc(s["v_lo"], 1)

            def q_low(b, c):
                dve.wait_ge(s["q_hi"], C * b + c + 1)
                low(qT[:, 1, c, :], x_bank[c][:, :], qT[:, 0, c, :]).then_inc(s["q_lo"], 1)

            def row_max(b, i):
                dve.wait_ge(s["scores_done"], T * b + i + 1)
                nc.vector.tensor_reduce(neg_max[:, i:i + 1], sc_bank[i % 2][:, 0:(i + 1) * P], AX.X, ALU.max,
                                        negate=True).then_inc(s["max_done"], 1)

            def p_low(b, i):
                dve.wait_ge(s["pT_hi"], T * b + i + 1)
                n = (i + 1) * P
                low(pT[:, i % 2, 1, 0:n], pt_bank[i % 2][:, 0:n], pT[:, i % 2, 0, 0:n]).then_inc(s["pT_lo"], 1)

            def invert(b, i):
                dve.wait_ge(s["exp_done"], T * b + i + 1)
                if not isinstance(b, int) or b > 0:
                    dve.wait_ge(s["attn_kept"], T * b + i + 1 - T)
                nc.vector.reciprocal(row_inv[:, i:i + 1], row_sum[:, i:i + 1]).then_inc(s["inv_done"], 1)

            def logits_max(b):
                dve.wait_ge(s["logits_kept"], b + 1)
                tiles = bass.ds(b * T, T)
                nc.vector.tensor_reduce(l_max[:, tiles], logits[:, tiles, :], AX.X, ALU.max).then_inc(s["logits_max"], 1)

            def logits_sum(b):
                dve.wait_ge(s["route_exp"], b + 1)
                tiles = bass.ds(b * T, T)
                nc.vector.tensor_reduce(l_sum[:, tiles], rb[:, tiles, :], AX.X, ALU.add).then_inc(s["inv_part"], 1)

            def logits_inv(b):
                dve.wait_ge(s["inv_part"], b + 1)
                tiles = bass.ds(b * T, T)
                nc.vector.reciprocal(l_inv[:, tiles], l_sum[:, tiles]).then_inc(s["inv_sum"], 1)

            def route(b, k):
                dve.wait_ge(s["route"], 2 + ROUTE * b + k)
                tiles = bass.ds(b * T, T)
                sums, scores = gs[:, tiles, :], rs[:, tiles, :]
                expert = 0 if k < 12 else 1
                if k == 0:
                    dve.wait_ge(s["scored"], 3 * (b + 1))
                if k < 2:
                    ins = nc.vector.tensor_tensor(beats[:, :, :, k, :], sums.unsqueeze(2).to_broadcast([P, T, G, G]),
                                                  sums.unsqueeze(3).to_broadcast([P, T, G, G]), (ALU.is_gt, ALU.is_equal)[k])
                elif k == 2:
                    ins = nc.vector.tensor_tensor(beats[:, :, :, 1, :], beats[:, :, :, 1, :],
                                                  before[:, :, :].unsqueeze(1).to_broadcast([P, T, G, G]), ALU.mult)
                elif k == 3:
                    ins = nc.vector.tensor_reduce(rank, beats.rearrange("p t g u h -> p t g (u h)"), AX.X, ALU.add)
                elif k == 4:
                    ins = nc.vector.tensor_scalar(rank, rank, 2.0, -DROPPED, ALU.is_ge, ALU.mult)
                elif k == 5:
                    ins = nc.vector.tensor_tensor(left.rearrange("p t (g u) -> p t g u", u=2), scores.rearrange("p t (g u) -> p t g u", u=2),
                                                  rank.unsqueeze(3).to_broadcast([P, T, G, 2]), ALU.add)
                elif k in (6, 12):
                    ins = nc.vector.tensor_reduce(largest, left, AX.X, ALU.max)
                elif k in (7, 13):
                    ins = nc.vector.tensor_tensor(best, left, largest.unsqueeze(2).to_broadcast([P, T, E]), ALU.is_equal)
                elif k in (8, 14):
                    ins = nc.vector.scalar_tensor_tensor(out=best, in0=best, scalar=-8.0, in1=iota_e[:, :].unsqueeze(1).to_broadcast([P, T, E]),
                                                         op0=ALU.mult, op1=ALU.add)
                elif k in (9, 15):
                    ins = nc.vector.tensor_reduce(e_of[:, tiles, expert], best, AX.X, ALU.min)
                elif k in (10, 16):
                    ins = nc.vector.tensor_tensor(picked[:, :, expert, :], iota_em[:, :].unsqueeze(1).to_broadcast([P, T, E]),
                                                  e_of[:, tiles, expert:expert + 1].to_broadcast([P, T, E]), ALU.is_equal)
                elif k == 11:
                    ins = nc.vector.scalar_tensor_tensor(out=left, in0=picked[:, :, 0, :], scalar=-DROPPED, in1=left, op0=ALU.mult, op1=ALU.add)
                elif k == 17:
                    ins = nc.vector.tensor_tensor(w_picked, picked, rc[:, tiles, :].unsqueeze(2).to_broadcast([P, T, K, E]), ALU.mult)
                elif k == 18:
                    ins = nc.vector.tensor_reduce(w_rows[:, bass.ds(b * RB, RB)].rearrange("p (t k) -> p t k", k=K), w_picked, AX.X, ALU.add)
                elif k == 19:
                    ins = nc.vector.tensor_tensor(at_least[:, tiles, :, :], iota_em[:, :].unsqueeze(1).unsqueeze(1).to_broadcast([P, T, K, E]),
                                                  e_of[:, tiles, :].unsqueeze(3).to_broadcast([P, T, K, E]), ALU.is_ge)
                ins.then_inc(s["route"], 1)

            for t in range(T):
                stats(0, t)
            mean_var(0)
            for t in range(T):
                scale_x(0, t)
            dve.wait_ge(s["wvg_hi"], 1)
            low(WVG_lo[:, :, 0:D], raw_qkv[:, 2, :, :], WVG_hi[:, :, 0:D])
            dve.wait_ge(s["wvg_hi"], 2)
            low(WVG_lo[:, :, D:VG], bank[2][:, 0:C * E].rearrange("p (c e) -> p c e", c=C),
                WVG_hi[:, :, D:VG]).then_inc(s["wvg_ready"], 1)
            dve.wait_ge(s["const_ready"], 6)
            nc.vector.tensor_scalar(upper[:, :], partition[:, :], float(PAIRS - 8), float(-PAIRS), ALU.is_ge, ALU.mult
                                    ).then_inc(s["route"], 1)
            dve.wait_ge(s["route"], 1)
            nc.vector.tensor_tensor(pair_of_partition[:, :], partition[:, :], upper[:, :], ALU.add).then_inc(s["route"], 1)
            x_low(0, 0)
            x_low(0, 1)
            stats(1, 0)
            stats(1, 1)
            dve.wait_ge(s["m_hi_ready"], 1)
            nc.vector.scalar_tensor_tensor(out=M_lo[:, :, :].rearrange("p c d -> p (c d)"), in0=bank[3][:, :], scalar=D ** -0.5,
                                           in1=M_hi[:, :, :].rearrange("p c d -> p (c d)").bitcast(F32),
                                           op0=ALU.mult, op1=ALU.subtract).then_inc(s["m_ready"], 1)
            stats(1, 2)
            stats(1, 3)
            mean_var(1)
            v_low(0, 0)
            v_low(0, 1)
            q_low(0, 0)
            scale_x(1, 0)
            scale_x(1, 1)
            q_low(0, 1)
            scale_x(1, 2)
            scale_x(1, 3)
            v_low(0, 2)
            v_low(0, 3)

            def step(b, norm=True):
                p = b + 1
                n = b + 2
                routes = not isinstance(b, int) or b > 0

                def also(*steps):
                    if routes:
                        for k in steps:
                            route(b - 1, k)

                if norm:
                    stats(n, 0)
                also(0)
                row_max(b, 0)
                also(1)
                logits_max(b)
                also(2)
                if norm:
                    stats(n, 1)
                row_max(b, 1)
                also(3)
                if norm:
                    stats(n, 2)
                x_low(p, 0)
                also(4, 5)
                x_low(p, 1)
                p_low(b, 0)
                also(6)
                row_max(b, 2)
                also(7)
                if norm:
                    stats(n, 3)
                logits_sum(b)
                also(8)
                if norm:
                    mean_var(n)
                also(9)
                v_low(p, 0)
                also(10)
                invert(b, 0)
                invert(b, 1)
                also(11)
                p_low(b, 1)
                also(12)
                row_max(b, 3)
                also(13)
                v_low(p, 1)
                also(14)
                p_low(b, 2)
                also(15, 16)
                q_low(p, 0)
                logits_inv(b)
                invert(b, 2)
                v_low(p, 2)
                p_low(b, 3)
                also(17)
                invert(b, 3)
                also(18)
                q_low(p, 1)
                v_low(p, 3)
                also(19)

            step(0)
            with dve.Fori(1, LOOP1) as b:
                step(b)
            step(B - 2, norm=False)

            b = B - 1
            sw_bank = [x_bank[0], x_bank[1], v_bank]

            def sw_low(n):
                dve.wait_ge(s["sw_hi"], n + 1)
                low(swT[:, 1, n, :, :].rearrange("p c d -> p (c d)"), sw_bank[n][:, :],
                    swT[:, 0, n, :, :].rearrange("p c d -> p (c d)")).then_inc(s["sw_ready"], 1)

            def also(*steps):
                for k in steps:
                    route(b - 1, k)

            row_max(b, 0)
            logits_max(b)
            also(0)
            row_max(b, 1)
            also(1)
            nc.vector.tensor_tensor(xn8[:, :, :], xT_hi_all[:, 0, :, 0:8].bitcast(F32), xT_lo_all[:, 0, :, 0:8].bitcast(F32),
                                    ALU.add).then_inc(s["xn8_ready"], 1)
            also(2)
            invert(b, 0)
            also(3)
            logits_sum(b)
            also(4)
            p_low(b, 0)
            logits_inv(b)
            row_max(b, 2)
            also(5)
            sw_low(0)
            also(6)
            invert(b, 1)
            also(7)
            p_low(b, 1)
            also(8)
            row_max(b, 3)
            also(9)
            sw_low(1)
            also(10)
            invert(b, 2)
            also(11, 12, 13, 14)
            p_low(b, 2)
            also(15)
            sw_low(2)
            also(16)
            invert(b, 3)
            also(17)
            p_low(b, 3)
            also(18, 19)
            for k in range(5):
                route(b, k)
            dve.wait_ge(s["a_split"], 1)
            low(A_T[:, PAIRS:P], x_bank[0][:, 0:PAIRS], A_T[:, 0:PAIRS]).then_inc(s["a_split"], 1)
            for k in range(5, ROUTE):
                route(b, k)
            dve.wait_ge(s["counted"], 1)
            nc.vector.tensor_reduce(ends[:, :], bank[5][:, 0:P].rearrange("p (r e) -> p e r", e=E), AX.X, ALU.add
                                    ).then_inc(s["route"], 1)
            dve.wait_ge(s["route"], ROUTED + 1)
            nc.vector.tensor_tensor(at_or_past, row_id[:, :, :].rearrange("p t k -> p (t k)").unsqueeze(2).to_broadcast([P, NR, E - 1]),
                                    ends[:, 0:E - 1].unsqueeze(1).to_broadcast([P, NR, E - 1]), ALU.is_ge).then_inc(s["route"], 1)
            dve.wait_ge(s["route"], ROUTED + 2)
            nc.vector.tensor_reduce(g_of, at_or_past, AX.X, ALU.add).then_inc(s["route"], 1)
            dve.wait_ge(s["route"], ROUTED + 3)
            nc.vector.scalar_tensor_tensor(out=pair_rows[:, :], in0=g_of, scalar=float(E),
                                           in1=e_of[:, :, :].rearrange("p t k -> p (t k)"),
                                           op0=ALU.mult, op1=ALU.add).then_inc(s["rows_ready"], 1)

            h1_bank, h3_bank, o_bank, bc_bank, g_bank, acc_bank = bank[0:2], bank[2:4], bank[4], bank[5], bank[6], bank[7]

            def pair_one_hots(i, g):
                if not isinstance(i, int) or i > 0:
                    dve.wait_ge(s[f"accumulated{g}"], i)
                elif g == 0:
                    dve.wait_ge(s["rows_ready"], 1)
                nc.vector.tensor_tensor(pair_one_hot[:, g, :, :], iota_pair[:, :].unsqueeze(1).to_broadcast([P, RG, PAIRS]),
                                        pair_rows[:, bass.ds(i * RB + g * RG, RG)].unsqueeze(2).to_broadcast([P, RG, PAIRS]),
                                        ALU.is_equal).then_inc(s["pair_one_hot_done"], 1)

            def one_hot(i, g):
                dve.wait_ge(s["bc_done"], 2 * i + g + 1)
                if not isinstance(i, int) or i > 0:
                    dve.wait_ge(s["gathered"], 2 * i + g - 1)
                nc.vector.tensor_scalar(one_hot_T[:, g, :], bc_bank[:, :], pair_of_partition[:, 0:1], None,
                                        ALU.is_equal).then_inc(s["one_hot_done"], 1)

            def h_mult(i, hc):
                dve.wait_ge(s["h_silu_done"], C * i + hc + 1)
                dve.wait_ge(s["h3_done"], C * i + hc + 1)
                if not isinstance(i, int) or i > 0:
                    dve.wait_ge(s["h_lo"], C * i + hc + 1 - C)
                nc.vector.tensor_tensor(h_full[:, hc, :], h3_bank[hc][:, :], h_silu[:, hc, :], ALU.mult).then_inc(s["h_mult_done"], 1)

            def h_low(i, hc):
                dve.wait_ge(s["h_hi"], C * i + hc + 1)
                low(hT[:, 1, hc, :], h_full[:, hc, :], hT[:, 0, hc, :]).then_inc(s["h_lo"], 1)

            def rows_low(i, g):
                dve.wait_ge(s["rows_hi"], 2 * i + g + 1)
                for j in range(RG):
                    ins = nc.vector.scalar_tensor_tensor(out=silu_split[:, g, j, 1, :], in0=row_silu[:, g, j, :],
                                                         scalar=w_rows[:, bass.ds(i * RB + g * RG + j, 1)],
                                                         in1=silu_split[:, g, j, 0, :].bitcast(F32),
                                                         op0=ALU.mult, op1=ALU.subtract)
                ins.then_inc(s["rows_lo"], 1)

            def gate_attn(i, half):
                dve.wait_ge(s["gate_done"], 2 * i + half + 1)
                b = sequence(i)
                g2 = gate[:, 2 * half:2 * half + 2, :]
                return nc.vector.tensor_tensor(g2, g2, attn_all[:, bass.ds(b * T + 2 * half, 2), :], ALU.mult)

            pair_one_hots(0, 0)
            h_mult(0, 0)
            one_hot(0, 0)
            one_hot(0, 1)
            h_low(0, 0)
            dve.wait_ge(s["tables_summed"], 8)
            nc.vector.tensor_copy(B_T[:, :], bank[7][:, 0:PAIRS]).then_inc(s["b_kept"], 1)
            h_mult(0, 1)
            rows_low(0, 0)
            h_low(0, 1)
            pair_one_hots(0, 1)

            def step2(i):
                one_hot(i, 0)
                rows_low(i - 1, 1)
                gate_attn(i - 1, 0).then_inc(s["gated"], 1)
                one_hot(i, 1)
                h_mult(i, 0)
                pair_one_hots(i, 0)
                rows_low(i, 0)
                h_mult(i, 1)
                gate_attn(i - 1, 1).then_inc(s["gated"], 1)
                h_low(i, 0)
                pair_one_hots(i, 1)
                h_low(i, 1)

            with dve.Fori(1, B - 1) as i:
                step2(i)
            i = B - 1
            one_hot(i, 0)
            pair_one_hots(i, 0)
            rows_low(i - 1, 1)
            one_hot(i, 1)
            h_mult(i, 0)
            pair_one_hots(i, 1)
            rows_low(i, 0)
            gate_attn(i - 1, 0).then_inc(s["gated"], 1)
            rows_low(i, 1)
            h_mult(i, 1)
            dve.wait_ge(s["accumulated0"], B)
            dve.wait_ge(s["accumulated1"], B)
            nc.vector.tensor_reduce(sum_w[0:PAIRS, :], acc_bank[0:PAIRS, 0:2 * H].rearrange("p (h d) -> p d h", h=2),
                                    AX.X, ALU.add).then_inc(s["sum_ready"], 1)
            dve.wait_ge(s["sum_turned"], 1)
            nc.vector.tensor_tensor(pair_out, bc_bank[:, 0:PAIRS], B_T[:, :], ALU.mult).then_inc(s["pairs_ready"], 1)
            gate_attn(i - 1, 1).then_inc(s["gated"], 1)
            h_low(i, 0)
            h_low(i, 1)
            dve.wait_ge(s["x_loaded"], 16 * (2 * B - 1))
            def times_attn(n):
                tiles = LAST_PIECES[n]
                if n == 0:
                    dve.wait_ge(s["gate_done"], 2 * i + 1)
                else:
                    dve.wait_ge(s["last_gate_done"], n)
                nc.vector.tensor_tensor(gate[:, tiles, :], gate[:, tiles, :], attn_all[:, tiles, :], ALU.mult).then_inc(s["last_gated"], 1)

            def plus_x(n):
                tiles = LAST_PIECES[n]
                slot = x_ring[:, i % 2, tiles, :]
                dve.wait_ge(s["last_gated"], n + 1)
                nc.vector.tensor_tensor(slot, slot, gate[:, tiles, :], ALU.add).then_inc(s["last_summed"], 1)

            times_attn(0)
            times_attn(1)
            plus_x(1)
            times_attn(2)
            plus_x(2)


NAMES = ["L0_attn_x", "L0_attn_WQ", "L0_attn_WK", "L0_attn_WV", "L0_ffn_w_gate", "L0_ffn_w1", "L0_ffn_w2", "L0_ffn_w3",
         "L0_ffn_sw1", "L0_ffn_sw2", "L0_ffn_sw3", "L0_ffn_expert_bias"]


def kernel(**inputs):
    import numpy as np
    import concourse.bacc as bacc
    from concourse.bass_utils import run_bass_kernel_spmd

    nc = bacc.Bacc("TRN2", target_bir_lowering=False, num_devices=1)
    arrays, args = {}, []
    for name in NAMES:
        a = np.ascontiguousarray(inputs[name])
        arrays[f"in_{name}"] = a
        args.append(nc.dram_tensor(f"in_{name}", a.shape, mybir.dt.from_np(a.dtype), kind="ExternalInput").ap())
    out = nc.dram_tensor("out", inputs["L0_attn_x"].shape, F32, kind="ExternalOutput").ap()
    build(nc, *args, out)
    r = run_bass_kernel_spmd(nc, [arrays], core_ids=[0])
    return r.results[0]["out"]
```
